# Optimizing a Trainium2 kernel written in Bass

```python
import numpy as np
import jax
import jax.numpy as jnp

def _softmax(x, axis=-1):
    return jax.nn.softmax(x, axis=axis)

def _gelu(x):
    return jax.nn.gelu(x, approximate=True)

def _silu(x):
    return jax.nn.silu(x)

def _sigmoid(x):
    return jax.nn.sigmoid(x)

def _layernorm(x, axis=-1, eps=1e-05):
    m = jnp.mean(x, axis=axis, keepdims=True)
    v = jnp.var(x, axis=axis, keepdims=True)
    return (x - m) / jnp.sqrt(v + eps)

def _scatter_add(tgt, idx, src, axis=0):
    return tgt.at[idx].add(src)

def _segment_sum(src, seg, n):
    return jax.ops.segment_sum(src, seg, n)
kernel_name = 'mk_adaln_attn_ffn_d1_seqx_r8_05dfe0'

def setup_inputs(seed: int=0):
    np.random.seed(seed)
    _w = jnp.asarray

    def _rec_inputs():
        import jax
        import jax.numpy as jnp
        _rk = jax.random.key(seed)
        x = -7.109e-05 + 0.9999 * jax.random.normal(jax.random.fold_in(_rk, 1), (32, 128, 128), jnp.float32)
        _lenS = 128 - jax.random.randint(jax.random.fold_in(_rk, 7), (32,), 0, max(1, 128 // 4) + 1, jnp.int32)
        _lenS2 = 128 - jax.random.randint(jax.random.fold_in(_rk, 8), (32,), 0, max(1, 128 // 4) + 1, jnp.int32)
        cond_512 = 0.0061147 + 1.02565 * jax.random.normal(jax.random.fold_in(_rk, 11), (32, 64), jnp.float32)
        return (x, cond_512)
    x, cond_512 = _rec_inputs()

    def _L0_cond_setup():
        import jax, jax.numpy as jnp
        import numpy as np
        W_DIM = 64
        CLAMP = 256.0
        key = jax.random.key(seed)
        ks = jax.random.split(key, 6)
        B, L, C = (8, 1024, 128)
        return {'x': jax.random.normal(ks[0], (B, L, C), dtype=jnp.float32), 'w': jax.random.normal(ks[1], (B, W_DIM), dtype=jnp.float32), 'weight': jax.random.normal(ks[2], (C, C), dtype=jnp.float32), 'bias': jax.random.normal(ks[3], (C,), dtype=jnp.float32), 'affine_w': jax.random.normal(ks[4], (C, W_DIM), dtype=jnp.float32), 'affine_b': jnp.ones((C,), dtype=jnp.float32)}
    _L0_cond_all = _L0_cond_setup()
    _L0_cond_in = {k: v for k, v in _L0_cond_all.items() if k in ('weight', 'bias', 'affine_w', 'affine_b')}
    del _L0_cond_all

    def _L0_attn_setup():
        import jax, jax.numpy as jnp
        import numpy as np
        DIM = 128
        BATCH = 4
        SEQ = 512
        key = jax.random.key(seed)
        ks = jax.random.split(key, 5)
        s = 1.0 / np.sqrt(DIM)
        x = jax.random.normal(ks[0], (BATCH, SEQ, DIM), dtype=jnp.float32)
        W_in = jax.random.uniform(ks[1], (DIM, DIM), jnp.float32, -s, s)
        b_in = jax.random.uniform(ks[2], (DIM,), jnp.float32, -s, s)
        W_out = jax.random.uniform(ks[3], (DIM, DIM), jnp.float32, -s, s)
        b_out = jax.random.uniform(ks[4], (DIM,), jnp.float32, -s, s)
        decay = jnp.float32(0.25)
        mix = jnp.float32(0.5)
        return {'x': x, 'W_in': W_in, 'b_in': b_in, 'W_out': W_out, 'b_out': b_out, 'decay': decay, 'mix': mix}
    _L0_attn_all = _L0_attn_setup()
    _L0_attn_in = {k: v for k, v in _L0_attn_all.items() if k in ('W_in', 'b_in', 'W_out', 'b_out', 'decay', 'mix')}
    del _L0_attn_all

    def _L0_cond2_setup():
        import jax, jax.numpy as jnp
        import numpy as np
        import math
        HEAD_NUM = 16
        EPS = 1e-08

        def modulated_linear(x, s, aff_w, aff_b, w, b):
            style = s @ aff_w.T + aff_b
            w_mod = w[None, :, :] * style[:, None, :]
            demod = jax.lax.rsqrt(jnp.sum(w_mod * w_mod, axis=2) + EPS)
            w_mod = w_mod * demod[:, :, None]
            return jnp.einsum('bni,boi->bno', x, w_mod) + b
        key = jax.random.key(seed)
        ks = jax.random.split(key, 6)
        B, N, F, S = (8, 128, 128, 64)
        return {'x': jax.random.normal(ks[0], (B, N, F), dtype=jnp.float32), 's': jax.random.normal(ks[1], (B, S), dtype=jnp.float32), 'k_aff_w': jax.random.normal(ks[2], (F, S), dtype=jnp.float32) * 0.02, 'k_aff_b': jnp.ones((F,), dtype=jnp.float32), 'k_w': jax.random.normal(ks[3], (F, F), dtype=jnp.float32) * 0.02, 'k_b': jnp.zeros((F,), dtype=jnp.float32), 'o_aff_w': jax.random.normal(ks[4], (F, S), dtype=jnp.float32) * 0.02, 'o_aff_b': jnp.ones((F,), dtype=jnp.float32), 'o_w': jax.random.normal(ks[5], (F, F), dtype=jnp.float32) * 0.02, 'o_b': jnp.zeros((F,), dtype=jnp.float32)}
    _L0_cond2_all = _L0_cond2_setup()
    _L0_cond2_in = {k: v for k, v in _L0_cond2_all.items() if k in ('k_aff_w', 'k_aff_b', 'k_w', 'k_b', 'o_aff_w', 'o_aff_b', 'o_w', 'o_b')}
    del _L0_cond2_all

    def _L0_ffn_setup():
        import jax, jax.numpy as jnp
        import numpy as np
        NUM_EXPERTS = 8
        N_EMBD = 128
        D_FF = 4 * N_EMBD
        B, S = (4, 256)
        key = jax.random.key(seed)
        ks = jax.random.split(key, 6)
        x = jax.random.normal(ks[0], (B, S, N_EMBD), dtype=jnp.float32)
        gate_w = jax.random.normal(ks[1], (N_EMBD, NUM_EXPERTS), dtype=jnp.float32) * 0.02
        w1 = jax.random.normal(ks[2], (NUM_EXPERTS, N_EMBD, D_FF), dtype=jnp.float32) * 0.02
        b1 = jnp.zeros((NUM_EXPERTS, D_FF), dtype=jnp.float32)
        w2 = jax.random.normal(ks[3], (NUM_EXPERTS, D_FF, N_EMBD), dtype=jnp.float32) * 0.02
        b2 = jnp.zeros((NUM_EXPERTS, N_EMBD), dtype=jnp.float32)
        return {'x': x, 'gate_w': gate_w, 'w1': w1, 'b1': b1, 'w2': w2, 'b2': b2}
    _L0_ffn_all = _L0_ffn_setup()
    _L0_ffn_in = {k: v for k, v in _L0_ffn_all.items() if k in ('gate_w', 'w1', 'b1', 'w2', 'b2')}
    del _L0_ffn_all
    return {'x': x, 'cond_512': cond_512, 'L0_cond_weight': _L0_cond_in['weight'], 'L0_cond_bias': _L0_cond_in['bias'], 'L0_cond_affine_w': _L0_cond_in['affine_w'], 'L0_cond_affine_b': _L0_cond_in['affine_b'], 'L0_attn_W_in': _L0_attn_in['W_in'], 'L0_attn_b_in': _L0_attn_in['b_in'], 'L0_attn_W_out': _L0_attn_in['W_out'], 'L0_attn_b_out': _L0_attn_in['b_out'], 'L0_attn_decay': _L0_attn_in['decay'], 'L0_attn_mix': _L0_attn_in['mix'], 'L0_cond2_k_aff_w': _L0_cond2_in['k_aff_w'], 'L0_cond2_k_aff_b': _L0_cond2_in['k_aff_b'], 'L0_cond2_k_w': _L0_cond2_in['k_w'], 'L0_cond2_k_b': _L0_cond2_in['k_b'], 'L0_cond2_o_aff_w': _L0_cond2_in['o_aff_w'], 'L0_cond2_o_aff_b': _L0_cond2_in['o_aff_b'], 'L0_cond2_o_w': _L0_cond2_in['o_w'], 'L0_cond2_o_b': _L0_cond2_in['o_b'], 'L0_ffn_gate_w': _L0_ffn_in['gate_w'], 'L0_ffn_w1': _L0_ffn_in['w1'], 'L0_ffn_b1': _L0_ffn_in['b1'], 'L0_ffn_w2': _L0_ffn_in['w2'], 'L0_ffn_b2': _L0_ffn_in['b2']}

def reference(x, cond_512, L0_cond_weight, L0_cond_bias, L0_cond_affine_w, L0_cond_affine_b, L0_attn_W_in, L0_attn_b_in, L0_attn_W_out, L0_attn_b_out, L0_attn_decay, L0_attn_mix, L0_cond2_k_aff_w, L0_cond2_k_aff_b, L0_cond2_k_w, L0_cond2_k_b, L0_cond2_o_aff_w, L0_cond2_o_aff_b, L0_cond2_o_w, L0_cond2_o_b, L0_ffn_gate_w, L0_ffn_w1, L0_ffn_b1, L0_ffn_w2, L0_ffn_b2):
    import jax
    import jax.numpy as jnp

    def _L0_cond_ref(x, w, weight, bias, affine_w, affine_b):
        import jax, jax.numpy as jnp
        import numpy as np
        W_DIM = 64
        CLAMP = 256.0
        B, L, C = x.shape
        gain = 1.0 / np.sqrt(W_DIM).astype(np.float32)
        styles = w @ (affine_w * gain).T + affine_b
        ws = weight[None, :, :] * styles[:, None, :]
        dcoefs = jax.lax.rsqrt(jnp.sum(ws * ws, axis=2) + 1e-08)
        xm = x * styles[:, None, :]
        y = jnp.einsum('blc,oc->blo', xm, weight)
        y = y * dcoefs[:, None, :]
        y = jnp.clip(y + bias, -CLAMP, CLAMP)
        return y

    def _L0_attn_ref(x, W_in, b_in, W_out, b_out, decay, mix):
        import jax, jax.numpy as jnp
        import numpy as np
        DIM = 128
        BATCH = 4
        SEQ = 512
        shifted = jnp.pad(x, ((0, 0), (1, 0), (0, 0)))[:, :-1]
        inp = mix * x + (1.0 - mix) * shifted
        h = jax.nn.relu(jnp.einsum('bsd,ed->bse', inp, W_in) + b_in)

        def step(state, h_t):
            state = state * decay + h_t
            return (state, state)
        h_t_major = jnp.swapaxes(h, 0, 1)
        _, states = jax.lax.scan(step, jnp.zeros((x.shape[0], x.shape[2]), x.dtype), h_t_major)
        states = jnp.swapaxes(states, 0, 1)
        return jnp.einsum('bsd,ed->bse', states, W_out) + b_out

    def _L0_cond2_ref(x, s, k_aff_w, k_aff_b, k_w, k_b, o_aff_w, o_aff_b, o_w, o_b):
        import jax, jax.numpy as jnp
        import numpy as np
        import math
        HEAD_NUM = 16
        EPS = 1e-08

        def modulated_linear(x, s, aff_w, aff_b, w, b):
            style = s @ aff_w.T + aff_b
            w_mod = w[None, :, :] * style[:, None, :]
            demod = jax.lax.rsqrt(jnp.sum(w_mod * w_mod, axis=2) + EPS)
            w_mod = w_mod * demod[:, :, None]
            return jnp.einsum('bni,boi->bno', x, w_mod) + b
        B, N, F = x.shape
        H = HEAD_NUM
        D = F // H
        kx = modulated_linear(x, s, k_aff_w, k_aff_b, k_w, k_b)
        kx = kx.reshape(B, N, H, D)
        q = k = v = kx
        scores = jnp.einsum('bnhd,bnjd->bnhj', q, k) / math.sqrt(D)
        A = jax.nn.softmax(scores, axis=-1)
        out = jnp.einsum('bnhj,bnjd->bnhd', A, v).reshape(B, N, F)
        out = modulated_linear(out, s, o_aff_w, o_aff_b, o_w, o_b)
        return out

    def _L0_ffn_ref(x, gate_w, w1, b1, w2, b2):
        import jax, jax.numpy as jnp
        import numpy as np
        NUM_EXPERTS = 8
        N_EMBD = 128
        D_FF = 4 * N_EMBD
        B, S = (4, 256)
        Bb, Ss, D = x.shape
        x_flat = x.reshape(-1, D)
        router_logits = x_flat @ gate_w
        router_probs = jax.nn.softmax(router_logits, axis=-1)
        expert_idx = jnp.argmax(router_probs, axis=-1)
        expert_w = jnp.take_along_axis(router_probs, expert_idx[:, None], axis=1)[:, 0]
        out = jnp.zeros_like(x_flat)
        for e in range(NUM_EXPERTS):
            h = jax.nn.gelu(x_flat @ w1[e] + b1[e], approximate=False)
            y = h @ w2[e] + b2[e]
            sel = expert_idx == e
            out = out + jnp.where(sel, expert_w, 0.0)[:, None] * y
        return out.reshape(Bb, Ss, D)
    x = x + _L0_attn_ref(_L0_cond_ref(x, cond_512, L0_cond_weight, L0_cond_bias, L0_cond_affine_w, L0_cond_affine_b), L0_attn_W_in, L0_attn_b_in, L0_attn_W_out, L0_attn_b_out, L0_attn_decay, L0_attn_mix)
    x = x + _L0_ffn_ref(_L0_cond2_ref(x, cond_512, L0_cond2_k_aff_w, L0_cond2_k_aff_b, L0_cond2_k_w, L0_cond2_k_b, L0_cond2_o_aff_w, L0_cond2_o_aff_b, L0_cond2_o_w, L0_cond2_o_b), L0_ffn_gate_w, L0_ffn_w1, L0_ffn_b1, L0_ffn_w2, L0_ffn_b2)
    return x

_drawn_inputs = setup_inputs


def setup_inputs(seed=0):
    import zlib

    import numpy as np

    out = dict(_drawn_inputs(seed))
    spreads = {'L0_cond_affine_b': (1.0, 0.6),
     'L0_cond2_k_aff_b': (1.0, 0.6),
     'L0_cond2_k_b': (0.0, 0.8),
     'L0_cond2_o_aff_b': (1.0, 0.6),
     'L0_cond2_o_b': (0.0, 0.8),
     'L0_ffn_b1': (0.0, 0.8),
     'L0_ffn_b2': (0.0, 0.531)}
    factors = {'L0_cond2_k_aff_w': 8.0,
     'L0_cond2_k_w': 3.545,
     'L0_cond2_o_aff_w': 8.0,
     'L0_cond2_o_w': 3.476,
     'L0_ffn_gate_w': 3.476,
     'L0_ffn_w1': 8.0,
     'L0_ffn_w2': 7.396}
    for name, (base, spread) in spreads.items():
        noise = np.random.default_rng([zlib.crc32(name.encode()), seed]).standard_normal(out[name].shape)
        drawn = base * np.exp(spread * noise) if base else spread * noise
        out[name] = jnp.asarray(drawn.astype(out[name].dtype))
    for name, factor in factors.items():
        out[name] = (out[name] * factor).astype(out[name].dtype)
    return out
```

```python
from contextlib import ExitStack

import concourse.bass as bass
from concourse import mybir

F32 = mybir.dt.float32
U32 = mybir.dt.uint32
ALU = mybir.AluOpType
ACT = mybir.ActivationFunctionType
AX = mybir.AxisListType.X

P = 128
CLAMP = 256.0
EPS = 1e-8


def adaln_attn_ffn(
    nc, x, cond, cw, c_bias, c_affw, c_affb, w_in, b_in, w_out, b_out, decay, mix,
    k_affw, k_affb, k_w, k_b, o_affw, o_affb, o_w, o_b, gate_w, w1, b1, w2, b2, out,
):
    B, L, C = x.shape
    WD = cond.shape[1]
    NE, _, F = w1.shape
    H, D = 16, C // 16
    assert L == P and C == P and D == 8
    G = 4
    GT = G * L
    NG = B // G
    NO = H // 2 + 1
    WRAP = H // 2
    UW = WRAP + H
    KQ = 4
    FK = F // P
    T = B * L
    CAP = T + P
    NS = (T + NE * (P - 1)) // P
    RW = 2 * C + 2
    CZ, CX, CWT, CID = 0, C, 2 * C, 2 * C + 1
    SKIP = 2 * T

    xg = x.rearrange("(g k) t c -> g t k c", k=G)
    out_rows = out.rearrange("b t c -> (b t) c")
    rows_dram = nc.dram_tensor("expert_rows", (NE * CAP + P, RW), F32, kind="Internal").ap()

    with ExitStack() as ctx:
        def sb(name, shape, dt=F32):
            return ctx.enter_context(nc.sbuf_tensor(name, shape, dt))

        def sem(name):
            return ctx.enter_context(nc.semaphore(name))

        bank = [ctx.enter_context(nc.psum_tensor(f"bank{i}", [P, 512], F32)) for i in range(8)]
        ps_a, ps_b, ps_av, ps_c, ps_d, ps_l = bank[:6]
        ps_h, ps_hT, ps_z, ps_y = bank[0:3], bank[3:6], bank[6], bank[7]

        ident = sb("ident", [P, P])
        lower = sb("lower", [P, P])
        ones = sb("ones", [P, P])
        iota_e = sb("iota_e", [P, G, NE])
        ecap = sb("ecap", [P, NE])
        iota_k = sb("iota_k", [P, NE, B])
        iota_i = sb("iota_i", [P, NS, NE])
        tokid = sb("tokid", [P, B])
        tail = sb("tail", [P, RW])
        mats = sb("mats", [P, 5, P])
        matsT = sb("matsT", [P, 5, P])
        affs = sb("affs", [P, 3, WD])
        affsT = sb("affsT", [WD, 3, P])
        condt = sb("condt", [B, WD])
        condT = sb("condT", [WD, B])
        vec = sb("vec", [P, 8])
        scal = sb("scal", [P, 4])
        decayt = sb("decayt", [P, L])
        styles = sb("styles", [P, 3, B])
        styles2 = sb("styles2", [P, 3, B])
        sqT = sb("sqT", [P, 3, P])
        var = sb("var", [P, 3, B])
        root = sb("root", [P, 3, B])
        inv = sb("inv", [P, 3, B])
        newt = sb("newt", [P, 3, B])
        demod = sb("demod", [P, 3, B])
        gatew = sb("gatew", [P, NE])
        w1s = sb("w1s", [P, NE, F])
        w2s = sb("w2s", [P, NE, FK, C])
        b1s = sb("b1s", [P, NE, F])
        b2s = sb("b2s", [P, NE, C])

        x_in = [sb(f"x_in{p}", [P, G, C]) for p in range(2)]
        xT = sb("xT", [P, GT])
        xm = sb("xm", [P, GT])
        yaff = sb("yaff", [P, GT])
        ypad = sb("ypad", [P, G, L + 1])
        ymix = sb("ymix", [P, GT])
        inp = sb("inp", [P, GT])
        hT = sb("hT", [P, GT])
        stT = sb("stT", [P, GT])
        x2T = sb("x2T", [P, GT])
        x2tok = sb("x2tok", [P, B, C])
        x2s = sb("x2s", [P, GT])
        kxT = sb("kxT", [P, GT])
        kext = [sb(f"kext{p}", [P, G, 2 * C]) for p in range(2)]
        qk = sb("qk", [P, NO, G, C])
        U = sb("U", [P, NO, G, UW])
        mx = sb("mx", [P, 3, G * H])
        sc = sb("sc", [P, H, G, H])
        e = sb("e", [P, H, G, H])
        esum = sb("esum", [P, G * H])
        rinv = sb("rinv", [P, G * H])
        av = [sb(f"av{c}", [P, KQ, GT]) for c in range(H // KQ)]
        att = sb("att", [P, GT])
        attT = sb("attT", [P, GT])
        zT = sb("zT", [P, GT])
        rows = [sb(f"rows{p}", [P, G, RW]) for p in range(2)]
        lmax = sb("lmax", [P, G])
        ld = sb("ld", [P, G, NE])
        le = sb("le", [P, G, NE])
        lsum = sb("lsum", [P, G])
        hit = sb("hit", [P, G, NE])
        score = sb("score", [P, G, NE])
        smin = sb("smin", [P, G])
        onehot = sb("onehot", [P, G, NE])
        rank = sb("rank", [P, G, NE])
        mine = sb("mine", [P, G, NE])
        posf = sb("posf", [P, G])
        pos = [sb(f"pos{p}", [P, G], U32) for p in range(2)]
        base = sb("base", [P, NE])
        cnt = sb("cnt", [P, NE])
        more = sb("more", [P, NE, B])
        ntile = sb("ntile", [P, NE])
        cum = sb("cum", [P, NE])
        past = sb("past", [P, NS, NE])
        pastn = sb("pastn", [P, NS, NE])
        tabf = sb("tabf", [P, 3, NS])
        tab = sb("tab", [P, 3, NS], U32)
        rt = [sb(f"rt{u}", [P, RW]) for u in range(3)]
        zt = [sb(f"zt{u}", [P, P]) for u in range(3)]
        hb, hg, hgT = ([qk[:, 3 * j + u, :, :].rearrange("p k c -> p (k c)") for u in range(3)] for j in range(3))
        yb = [inp[:, u * C:(u + 1) * C] for u in range(3)]
        orow = [x2s[:, u * C:(u + 1) * C] for u in range(3)]
        oid = [sb(f"oid{u}", [P, 1], U32) for u in range(3)]

        s_consts = sem("consts")
        s_selz = sem("selz")
        s_mats_ld = sem("mats_ld")
        s_aff_ld = sem("aff_ld")
        s_vec_ld = sem("vec_ld")
        s_scal_ld = sem("scal_ld")
        s_exp_ld = sem("exp_ld")
        s_setT_ps = sem("setT_ps")
        s_setT_sb = sem("setT_sb")
        s_aux_ps = sem("aux_ps")
        s_aux_sb = sem("aux_sb")
        s_sty_ps = sem("sty_ps")
        s_sty_sb = sem("sty_sb")
        s_sq_sb = sem("sq_sb")
        s_dem_ps = sem("dem_ps")
        s_var_sb = sem("var_sb")
        s_root_sb = sem("root_sb")
        s_dchain = sem("dchain")
        s_setup_done = sem("setup_done")
        s_xT_ps = sem("xT_ps")
        s_xT_sb = sem("xT_sb")
        s_xm_sb = sem("xm_sb")
        s_y_ps = sem("y_ps")
        s_y_aff = sem("y_aff")
        s_y_clip = sem("y_clip")
        s_y_mix = sem("y_mix")
        s_inp_sb = sem("inp_sb")
        s_h_ps = sem("h_ps")
        s_h_sb = sem("h_sb")
        s_st_sb = sem("st_sb")
        s_o_ps = sem("o_ps")
        s_x2_sb = sem("x2_sb")
        s_x2t_ps = sem("x2t_ps")
        s_x2tok_sb = sem("x2tok_sb")
        s_x2s_sb = sem("x2s_sb")
        s_kx_ps = sem("kx_ps")
        s_kxT_sb = sem("kxT_sb")
        s_kt_ps = sem("kt_ps")
        s_kext_sb = sem("kext_sb")
        s_qk_sb = sem("qk_sb")
        s_u_sb = sem("u_sb")
        s_u_wrap = sem("u_wrap")
        s_m_part = sem("m_part")
        s_m_sb = sem("m_sb")
        s_sc_sb = sem("sc_sb")
        s_e_sb = sem("e_sb")
        s_esum_sb = sem("esum_sb")
        s_rinv_sb = sem("rinv_sb")
        s_av_sb = sem("av_sb")
        s_av_ps = sem("av_ps")
        s_att_sb = sem("att_sb")
        s_at_ps = sem("at_ps")
        s_attT_sb = sem("attT_sb")
        s_z_ps = sem("z_ps")
        s_zT_sb = sem("zT_sb")
        s_zt_ps = sem("zt_ps")
        s_z_rows = sem("z_rows")
        s_lg_ps = sem("lg_ps")
        s_lmax_sb = sem("lmax_sb")
        s_ld_sb = sem("ld_sb")
        s_le_sb = sem("le_sb")
        s_lsum_sb = sem("lsum_sb")
        s_hit_sb = sem("hit_sb")
        s_score_sb = sem("score_sb")
        s_smin_sb = sem("smin_sb")
        s_oh_sb = sem("oh_sb")
        s_rank_ps = sem("rank_ps")
        s_rank_sb = sem("rank_sb")
        s_mine_sb = sem("mine_sb")
        s_posf_sb = sem("posf_sb")
        s_pos_sb = sem("pos_sb")
        s_base_sb = sem("base_sb")
        s_x2_rows = sem("x2_rows")
        s_rows_free = sem("rows_free")
        s_tab_sb = sem("tab_sb")
        s_tails_done = sem("tails_done")
        s_zero_done = sem("zero_done")
        s_zt2_ps = sem("zt2_ps")
        s_zt2_sb = sem("zt2_sb")
        s_h2_ps = sem("h2_ps")
        s_hb_sb = sem("hb_sb")
        s_hg_sb = sem("hg_sb")
        s_hgT_ps = sem("hgT_ps")
        s_hgT_sb = sem("hgT_sb")
        s_y2_ps = sem("y2_ps")
        s_yb_sb = sem("yb_sb")
        s_orow_sb = sem("orow_sb")
        s_oid_sb = sem("oid_sb")
        x_ld = [sem(f"x_ld{p}") for p in range(2)]
        scat = [sem(f"scat{p}") for p in range(2)]
        rt_ld = [sem(f"rt_ld{u}") for u in range(3)]
        o_out = [sem(f"o_out{u}") for u in range(3)]

        def due(n):
            return not isinstance(n, int) or n > 0

        def tiles(ap):
            return ap.rearrange("p (k t) -> p k t", k=G)

        def per_batch(table, j, g):
            return table[:, j, bass.ds(g * G, G)].unsqueeze(2).to_broadcast([P, G, L])

        def run_steps(eng, step):
            step(0, 0, True, False, False)
            step(1, 1, True, True, False)
            with eng.Fori(0, (NG - 2) // 2) as i:
                for u in range(2):
                    step(i * 2 + (2 + u), u, True, True, True)
            step(NG, 0, False, True, True)
            step(NG + 1, 1, False, False, True)

        block = ctx.enter_context(nc.Block())

        @block.sync
        def _(sp):
            for j, w in enumerate((cw, w_in, w_out, k_w, o_w)):
                sp.dma_start(mats[:, j, :], w).then_inc(s_mats_ld, 16)
            sp.dma_start(x_in[0][:, :, :], xg[0]).then_inc(x_ld[0], 16)
            sp.dma_start(x_in[1][:, :, :], xg[1]).then_inc(x_ld[1], 16)
            sp.dma_start(gatew[:, :], gate_w).then_inc(s_exp_ld, 16)
            sp.dma_start(w1s[:, :, :], w1.rearrange("e c f -> c e f")).then_inc(s_exp_ld, 16)
            sp.dma_start(w2s[:, :, :, :], w2.rearrange("e (k p) c -> p e k c", p=P)).then_inc(s_exp_ld, 16)
            sp.dma_start(b1s[:, :, :], b1.rearrange("(a e) f -> a e f", a=1).to_broadcast([P, NE, F])).then_inc(s_exp_ld, 16)
            sp.dma_start(b2s[:, :, :], b2.rearrange("(a e) f -> a e f", a=1).to_broadcast([P, NE, C])).then_inc(s_exp_ld, 16)
            with sp.Fori(0, (NG - 2) // 2) as i:
                for p in range(2):
                    sp.wait_ge(s_xT_ps, i * 2 + (1 + p))
                    sp.dma_start(x_in[p][:, :, :], xg[bass.ds(i * 2 + (2 + p), 1)].rearrange("a t k c -> (a t) k c")).then_inc(x_ld[p], 16)
            sp.wait_ge(s_consts, 1)
            sp.dma_start(rows_dram[NE * CAP:NE * CAP + P, :], tail[:, :]).then_inc(s_zero_done, 16)
            sp.wait_ge(s_tab_sb, 1)
            for ex in range(NE):
                r = sp.value_load(tab[0:1, 2, ex:ex + 1], min_val=ex * CAP, max_val=ex * CAP + T)
                sp.dma_start(rows_dram[bass.ds(r, P), :], tail[:, :]).then_inc(s_tails_done, 16)
            sp.wait_ge(s_zero_done, 16)
            sp.wait_ge(s_tails_done, 16 * NE)
            sp.wait_ge(s_rows_free, NG + 2)

            def load(i, u, first):
                r = sp.value_load(tab[0:1, 1, bass.ds(i, 1)], min_val=0, max_val=NE * CAP)
                if not first:
                    sp.wait_ge(s_orow_sb, i - 2)
                sp.dma_start(rt[u][:, :], rows_dram[bass.ds(r, P), :]).then_inc(rt_ld[u], 16)
            for u in range(3):
                load(u, u, True)
            with sp.Fori(1, NS // 3) as i:
                for u in range(3):
                    load(i * 3 + u, u, False)

        @block.gpsimd
        def _(gp):
            gp.memset(tail[:, :], 0.0).then_inc(s_selz, 1)
            gp.memset(ident[:, :], 0.0).then_inc(s_selz, 1)
            gp.memset(ones[:, :], 1.0).then_inc(s_selz, 1)
            gp.wait_ge(s_selz, 3)
            gp.memset(tail[:, CID:CID + 1], float(SKIP))
            gp.affine_select(out=ident[:, :], in_=ident[:, :], compare_op=ALU.not_equal, fill=1.0, base=0,
                             pattern=[[-1, P]], channel_multiplier=1)
            gp.affine_select(out=lower[:, :], in_=ones[:, :], compare_op=ALU.is_gt, fill=0.0, base=0,
                             pattern=[[1, P]], channel_multiplier=-1)
            gp.iota(iota_e[:, :, :], pattern=[[0, G], [1, NE]], base=0, channel_multiplier=0, allow_small_or_imprecise_dtypes=True)
            gp.iota(ecap[:, :], pattern=[[CAP, NE]], base=0, channel_multiplier=0, allow_small_or_imprecise_dtypes=True)
            gp.iota(iota_k[:, :, :], pattern=[[0, NE], [P, B]], base=0, channel_multiplier=0, allow_small_or_imprecise_dtypes=True)
            gp.iota(iota_i[:, :, :], pattern=[[1, NS], [0, NE]], base=0, channel_multiplier=0, allow_small_or_imprecise_dtypes=True)
            gp.memset(ypad[:, :, 0:1], 0.0)
            gp.iota(tokid[:, :], pattern=[[L, B]], base=0, channel_multiplier=1, allow_small_or_imprecise_dtypes=True)
            gp.drain().then_inc(s_consts, 1)
            gp.drain().then_inc(s_rows_free, 2)
            gp.wait_ge(s_consts, 1)
            gp.wait_ge(s_setup_done, 1)

            def step(s, u, do_a, do_b, do_c):
                if do_a:
                    g = s
                    gp.wait_ge(s_xT_sb, g + 1)
                    gp.tensor_tensor(tiles(xm[:, :]), tiles(xT[:, :]), per_batch(styles, 0, g), ALU.mult).then_inc(s_xm_sb, 1)
                if do_c:
                    g = s - 2
                    gp.tensor_copy(rows[u][:, :, CX:CX + C], x2tok[:, bass.ds(g * G, G), :])
                    gp.tensor_copy(rows[u][:, :, CID:CID + 1], tokid[:, bass.ds(g * G, G)].unsqueeze(2)).then_inc(s_x2_rows, 1)
                if do_a:
                    g = s
                    gp.wait_ge(s_x2_sb, g + 1)
                    gp.tensor_tensor(tiles(x2s[:, :]), tiles(x2T[:, :]), per_batch(styles, 1, g), ALU.mult).then_inc(s_x2s_sb, 1)
                if do_c:
                    g = s - 2
                    gp.wait_ge(s_x2_rows, g + 1)
                    gp.wait_ge(s_z_rows, g + 1)
                    gp.wait_ge(s_pos_sb, g + 1)
                    gp.nop(nofuse=True)
                    for k in range(G):
                        gp.indirect_dma_start(rows_dram[:, :], bass.IndirectOffsetOnAxis(ap=pos[u][:, k:k + 1], axis=0),
                                              rows[u][:, k, :], None).then_inc(scat[u], 16)
                    gp.wait_ge(scat[u], (s - u) * (8 * G))
                    gp.nop(nofuse=True)
                    gp.drain().then_inc(s_rows_free, 1)
            run_steps(gp, step)

            def send(i, u, n):
                gp.wait_ge(s_orow_sb, i + 1)
                gp.wait_ge(s_oid_sb, i + 1)
                gp.nop(nofuse=True)
                gp.indirect_dma_start(out_rows, bass.IndirectOffsetOnAxis(ap=oid[u][:, 0:1], axis=0), orow[u], None,
                                      bounds_check=T - 1, oob_is_err=False).then_inc(o_out[u], 16)
            with gp.Fori(0, NS // 3) as i:
                for u in range(3):
                    send(i * 3 + u, u, i)
            for u in range(3):
                gp.wait_ge(o_out[u], 16 * (NS // 3))

        @block.tensor
        def _(pe):
            mm = nc.tensor.matmul

            def transpose4(dst, src):
                for k in range(G):
                    last = nc.tensor.transpose(dst[:, k * P:(k + 1) * P], src(k), ident[:, :])
                return last

            pe.wait_ge(s_consts, 1)
            pe.wait_ge(s_mats_ld, 80)
            transpose4(ps_a, lambda k: mats[:, k, :])
            nc.tensor.transpose(ps_b[:, 0:P], mats[:, 4, :], ident[:, :]).then_inc(s_setT_ps, 1)
            pe.wait_ge(s_aff_ld, 64)
            for j in range(3):
                nc.tensor.transpose(ps_av[0:WD, j * P:(j + 1) * P], affs[:, j, :], ident[:, :])
            nc.tensor.transpose(ps_c[0:WD, 0:B], condt[:, :], ident[0:B, 0:B]).then_inc(s_aux_ps, 1)
            pe.wait_ge(s_aux_sb, 1)
            for j in range(3):
                last = mm(ps_d[:, j * B:(j + 1) * B], affsT[:, j, :], condT[:, :], start=True, stop=True)
            last.then_inc(s_sty_ps, 1)
            pe.wait_ge(s_sq_sb, 1)
            for j in range(3):
                last = mm(ps_l[:, j * B:(j + 1) * B], sqT[:, j, :], styles2[:, j, :], start=True, stop=True)
            last.then_inc(s_dem_ps, 1)
            pe.wait_ge(s_setup_done, 1)
            pe.wait_ge(s_exp_ld, 80)

            def value_sums(g, c0, c1):
                for c in range(c0, c1):
                    pe.wait_ge(s_av_sb, g * (H // KQ) + (c + 1))
                    if c == 0:
                        if due(g):
                            pe.wait_ge(s_att_sb, g)
                    for o in range(KQ):
                        first, end = c == 0 and o == 0, c == H // KQ - 1 and o == KQ - 1
                        last = mm(ps_av[:, :], ident[:, :], av[c][:, o, :], start=first, stop=end)
                    last.then_inc(s_av_ps, 1)

            def step(s, u, do_a, do_b, do_c):
                ga, gb, gc = s, s - 1, s - 2
                if do_a:
                    pe.wait_ge(x_ld[u], (s - u) * 8 + 16)
                    if due(ga):
                        pe.wait_ge(s_kext_sb, ga)
                    transpose4(ps_a, lambda k: x_in[u][:, k, :]).then_inc(s_xT_ps, 1)
                    pe.wait_ge(s_xm_sb, ga + 1)
                    mm(ps_b[:, :], matsT[:, 0, :], xm[:, :], start=True, stop=True).then_inc(s_y_ps, 1)
                if do_c:
                    pe.wait_ge(s_att_sb, gc + 1)
                    transpose4(ps_c, lambda k: att[:, k * P:(k + 1) * P]).then_inc(s_at_ps, 1)
                    pe.wait_ge(s_attT_sb, gc + 1)
                    mm(ps_d[:, :], matsT[:, 4, :], attT[:, :], start=True, stop=True).then_inc(s_z_ps, 1)
                if do_a:
                    pe.wait_ge(s_inp_sb, ga + 1)
                    mm(ps_a[:, :], matsT[:, 1, :], inp[:, :], start=True, stop=True).then_inc(s_h_ps, 1)
                if do_c:
                    pe.wait_ge(s_zT_sb, gc + 1)
                    transpose4(ps_c, lambda k: zT[:, k * P:(k + 1) * P]).then_inc(s_zt_ps, 1)
                    for k in range(G):
                        last = mm(ps_l[:, k * NE:(k + 1) * NE], zT[:, k * P:(k + 1) * P], gatew[:, :], start=True, stop=True)
                    last.then_inc(s_lg_ps, 1)
                if do_a:
                    pe.wait_ge(s_st_sb, ga + 1)
                    mm(ps_b[:, :], matsT[:, 2, :], stT[:, :], start=True, stop=True).then_inc(s_o_ps, 1)
                if do_c:
                    pe.wait_ge(s_oh_sb, gc + 1)
                    oh = onehot[:, :, :].rearrange("p k e -> p (k e)")
                    mm(ps_l[:, 64:64 + G * NE], lower[:, :], oh, start=True, stop=False)
                    for k in range(1, G):
                        mm(ps_l[:, 64 + k * NE:64 + G * NE], ones[:, :], oh[:, 0:(G - k) * NE], start=False, stop=k == G - 1)
                    for k in range(G):
                        last = mm(ps_l[:, 128:128 + NE], ones[:, :], onehot[:, k, :], start=k == 0, stop=k == G - 1)
                    last.then_inc(s_rank_ps, 1)
                if do_b:
                    value_sums(gb, 0, 2)
                if do_a:
                    pe.wait_ge(s_x2_sb, ga + 1)
                    transpose4(ps_a, lambda k: x2T[:, k * P:(k + 1) * P]).then_inc(s_x2t_ps, 1)
                    pe.wait_ge(s_x2s_sb, ga + 1)
                    mm(ps_b[:, :], matsT[:, 3, :], x2s[:, :], start=True, stop=True).then_inc(s_kx_ps, 1)
                if do_b:
                    value_sums(gb, 2, 3)
                if do_a:
                    pe.wait_ge(s_kxT_sb, ga + 1)
                    transpose4(ps_a, lambda k: kxT[:, k * P:(k + 1) * P]).then_inc(s_kt_ps, 1)
                if do_b:
                    value_sums(gb, 3, 4)
            run_steps(pe, step)

            pe.wait_ge(s_tab_sb, 1)

            def z_transpose(q, u):
                pe.wait_ge(rt_ld[u], q * 16 + 16)
                if due(q * 3 + u):
                    pe.wait_ge(s_zt2_sb, q * 3 + u)
                nc.tensor.transpose(ps_z[:, 0:P], rt[u][:, CZ:CZ + C], ident[:, :]).then_inc(s_zt2_ps, 1)

            def up(q, u):
                i = q * 3 + u
                r = pe.value_load(tab[0:1, 0, bass.ds(i, 1)], min_val=0, max_val=NE - 1)
                pe.wait_ge(s_zt2_sb, i + 1)
                if due(i - 2):
                    pe.wait_ge(s_hb_sb, i - 2)
                mm(ps_h[u][:, :], zt[u][:, :], w1s[:, bass.ds(r, 1), :].rearrange("p a f -> p (a f)"),
                   start=True, stop=True).then_inc(s_h2_ps, 1)

            def turn(q, u):
                i = q * 3 + u
                pe.wait_ge(s_hg_sb, i + 1)
                transpose4(ps_hT[u], lambda k: hg[u][:, k * P:(k + 1) * P]).then_inc(s_hgT_ps, 1)

            def down(q, u):
                i = q * 3 + u
                r = pe.value_load(tab[0:1, 0, bass.ds(i, 1)], min_val=0, max_val=NE - 1)
                pe.wait_ge(s_hgT_sb, i + 1)
                if due(i):
                    pe.wait_ge(s_yb_sb, i)
                for k in range(FK):
                    last = mm(ps_y[:, 0:C], hgT[u][:, k * P:(k + 1) * P],
                              w2s[:, bass.ds(r, 1), k, :].rearrange("p a c -> p (a c)"), start=k == 0, stop=k == FK - 1)
                last.then_inc(s_y2_ps, 1)

            def back(q, u, n):
                return (q, u - n) if u >= n else (q - 1, u - n + 3)

            z_transpose(0, 0)
            for u in range(3):
                up(0, u)
                if u >= 1:
                    turn(0, u - 1)
                if u >= 2:
                    down(0, u - 2)
                if u < 2:
                    z_transpose(0, u + 1)
            z_transpose(1, 0)
            with pe.Fori(1, NS // 3 - 1) as q:
                for u in range(3):
                    up(q, u)
                    turn(*back(q, u, 1))
                    down(*back(q, u, 2))
                    z_transpose(*((q, u + 1) if u < 2 else (q + 1, 0)))
            q = NS // 3 - 1
            for u in range(3):
                up(q, u)
                turn(*back(q, u, 1))
                down(*back(q, u, 2))
                if u < 2:
                    z_transpose(q, u + 1)
            turn(q, 2)
            down(q, 1)
            down(q, 2)

        @block.scalar
        def _(act):
            a = nc.scalar.activation
            for j, v in enumerate((c_affw, k_affw, o_affw)):
                act.dma_start(affs[:, j, :], v).then_inc(s_aff_ld, 16)
            act.dma_start(condt[:, :], cond).then_inc(s_aff_ld, 16)
            for j, v in enumerate((c_affb, k_affb, o_affb, c_bias, b_in, b_out, k_b, o_b)):
                act.dma_start(vec[:, j:j + 1], v.rearrange("(p a) -> p a", a=1)).then_inc(s_vec_ld, 16)
            for j, v in enumerate((decay, mix)):
                act.dma_start(scal[:, j:j + 1], v.rearrange("(p a) -> p a", a=1).to_broadcast([P, 1])).then_inc(s_scal_ld, 16)
            act.wait_ge(s_setT_ps, 1)
            a(matsT[:, 0:4, :].rearrange("p j c -> p (j c)"), ps_a[:, :], ACT.Copy)
            a(matsT[:, 4, :], ps_b[:, 0:P], ACT.Copy).then_inc(s_setT_sb, 1)
            act.wait_ge(s_aux_ps, 1)
            a(condT[:, :], ps_c[0:WD, 0:B], ACT.Copy)
            a(affsT[:, :, :].rearrange("p j c -> p (j c)"), ps_av[0:WD, 0:3 * P], ACT.Copy).then_inc(s_aux_sb, 1)
            act.wait_ge(s_sty_ps, 1)
            act.wait_ge(s_vec_ld, 128)
            for j, gain in enumerate((float(WD) ** -0.5, 1.0, 1.0)):
                last = a(styles[:, j, :], ps_d[:, j * B:(j + 1) * B], ACT.Identity, bias=vec[:, j:j + 1], scale=gain)
            last.then_inc(s_sty_sb, 1)
            act.wait_ge(s_var_sb, 1)
            a(root[:, :, :], var[:, :, :], ACT.Sqrt).then_inc(s_root_sb, 1)
            act.wait_ge(s_setup_done, 1)

            def affine4(dst, src, scale_j, table, bias, g):
                for k in range(G):
                    last = a(dst[:, k * P:(k + 1) * P], src[:, k * P:(k + 1) * P], ACT.Identity,
                             scale=table[:, scale_j, bass.ds(g * G + k, 1)], bias=bias)
                return last

            def step(s, u, do_a, do_b, do_c):
                ga, gb, gc = s, s - 1, s - 2
                if do_a:
                    act.wait_ge(s_xT_ps, ga + 1)
                    a(xT[:, :], ps_a[:, :], ACT.Copy).then_inc(s_xT_sb, 1)
                    act.wait_ge(s_y_ps, ga + 1)
                    affine4(yaff, ps_b, 0, demod, vec[:, 3:4], ga).then_inc(s_y_aff, 1)
                if do_c:
                    act.wait_ge(s_at_ps, gc + 1)
                    affine4(attT, ps_c, 2, styles, 0.0, gc).then_inc(s_attT_sb, 1)
                    act.wait_ge(s_z_ps, gc + 1)
                    affine4(zT, ps_d, 2, demod, vec[:, 7:8], gc).then_inc(s_zT_sb, 1)
                if do_a:
                    act.wait_ge(s_h_ps, ga + 1)
                    a(hT[:, :], ps_a[:, :], ACT.Relu, bias=vec[:, 4:5]).then_inc(s_h_sb, 1)
                if do_c:
                    act.wait_ge(s_zt_ps, gc + 1)
                    act.wait_ge(s_rows_free, gc + 1)
                    a(rows[u][:, :, CZ:CZ + C], tiles(ps_c[:, :]), ACT.Copy).then_inc(s_z_rows, 1)
                if do_b:
                    act.wait_ge(s_sc_sb, gb + 1)
                    a(e[:, :, :, :], sc[:, :, :, :], ACT.Exp, scale=float(D) ** -0.5).then_inc(s_e_sb, 1)
                if do_c:
                    act.wait_ge(s_ld_sb, gc + 1)
                    a(le[:, :, :], ld[:, :, :], ACT.Exp).then_inc(s_le_sb, 1)
                if do_a:
                    act.wait_ge(s_x2t_ps, ga + 1)
                    a(x2tok[:, bass.ds(ga * G, G), :], tiles(ps_a[:, :]), ACT.Copy).then_inc(s_x2tok_sb, 1)
                    act.wait_ge(s_kx_ps, ga + 1)
                    affine4(kxT, ps_b, 1, demod, vec[:, 6:7], ga).then_inc(s_kxT_sb, 1)
                    act.wait_ge(s_kt_ps, ga + 1)
                    for r in range(2):
                        last = a(kext[u][:, :, r * C:(r + 1) * C], tiles(ps_a[:, :]), ACT.Copy)
                    last.then_inc(s_kext_sb, 1)
            run_steps(act, step)

            def z_copy(q, u):
                act.wait_ge(s_zt2_ps, q * 3 + (u + 1))
                a(zt[u][:, :], ps_z[:, 0:P], ACT.Copy).then_inc(s_zt2_sb, 1)

            def gelu(q, u):
                act.wait_ge(s_hb_sb, q * 3 + (u + 1))
                a(hg[u], hb[u], ACT.Gelu).then_inc(s_hg_sb, 1)
            z_copy(0, 0)
            with act.Fori(0, NS // 3 - 1) as q:
                for u in range(3):
                    z_copy(*((q, u + 1) if u < 2 else (q + 1, 0)))
                    gelu(q, u)
            q = NS // 3 - 1
            for u in range(3):
                if u < 2:
                    z_copy(q, u + 1)
                gelu(q, u)

        @block.vector
        def _(dve):
            v = nc.vector
            tt, ts = v.tensor_tensor, v.tensor_scalar

            chain = [0]

            def then(ins):
                chain[0] += 1
                ins.then_inc(s_dchain, 1)
                dve.wait_ge(s_dchain, chain[0])

            dve.wait_ge(s_consts, 1)
            v.tensor_copy(base[:, :], ecap[:, :]).then_inc(s_base_sb, 1)
            dve.wait_ge(s_scal_ld, 32)
            then(ts(decayt[:, :], ones[:, :], scal[:, 0:1], None, ALU.mult))
            then(ts(scal[:, 2:3], scal[:, 1:2], -1.0, 1.0, ALU.mult, ALU.add))
            dve.wait_ge(s_setT_sb, 1)
            dve.wait_ge(s_sty_sb, 1)
            tt(styles2[:, :, :], styles[:, :, :], styles[:, :, :], ALU.mult)
            tt(sqT[:, 0, :], matsT[:, 0, :], matsT[:, 0, :], ALU.mult)
            tt(sqT[:, 1:3, :], matsT[:, 3:5, :], matsT[:, 3:5, :], ALU.mult).then_inc(s_sq_sb, 1)
            dve.wait_ge(s_dem_ps, 1)
            ts(var[:, :, :].rearrange("p j b -> p (j b)"), ps_l[:, 0:3 * B], EPS, None, ALU.add).then_inc(s_var_sb, 1)
            dve.wait_ge(s_root_sb, 1)
            then(v.reciprocal(inv[:, :, :], root[:, :, :]))
            then(tt(newt[:, :, :], inv[:, :, :], inv[:, :, :], ALU.mult))
            then(tt(newt[:, :, :], newt[:, :, :], var[:, :, :], ALU.mult))
            then(ts(newt[:, :, :], newt[:, :, :], -0.5, 1.5, ALU.mult, ALU.add))
            tt(demod[:, :, :], inv[:, :, :], newt[:, :, :], ALU.mult).then_inc(s_setup_done, 1)

            def shifted(o1):
                return bass.AP(tensor=U, offset=o1 * G * UW + WRAP - o1,
                               ap=[[NO * G * UW, P], [G * UW - 1, H - NO], [UW, G], [1, H]])

            def heads(ap):
                return ap.rearrange("p (k h) -> p k h", k=G)

            def step(s, u, do_a, do_b, do_c):
                ga, gb, gc = s, s - 1, s - 2
                kx = kext[1 - u]
                if do_b:
                    dve.wait_ge(s_kext_sb, gb + 1)
                    q = bass.AP(tensor=kx, offset=0, ap=[[G * 2 * C, P], [0, NO], [2 * C, G], [1, C]])
                    qo = bass.AP(tensor=kx, offset=0, ap=[[G * 2 * C, P], [D, NO], [2 * C, G], [1, C]])
                    tt(qk[:, :, :, :], q, qo, ALU.mult).then_inc(s_qk_sb, 1)
                if do_c:
                    dve.wait_ge(s_av_ps, (gc + 1) * (H // KQ))
                    dve.wait_ge(s_rinv_sb, gc + 1)
                    tt(att[:, :].rearrange("p (h d) -> p h d", d=D), ps_av[:, :].rearrange("p (h d) -> p h d", d=D),
                       rinv[:, :].unsqueeze(2).to_broadcast([P, G * H, D]), ALU.mult).then_inc(s_att_sb, 1)
                if do_b:
                    dve.wait_ge(s_qk_sb, gb + 1)
                    v.reduce_sum(U[:, :, :, WRAP:UW], qk[:, :, :, :].rearrange("p o k (h d) -> p (o k) h d", d=D), AX).then_inc(s_u_sb, 1)
                if do_a:
                    dve.wait_ge(s_y_aff, ga + 1)
                    ts(ypad[:, :, 1:L + 1], tiles(yaff[:, :]), CLAMP, -CLAMP, ALU.min, ALU.max).then_inc(s_y_clip, 1)
                    dve.wait_ge(s_y_clip, ga + 1)
                    ts(tiles(ymix[:, :]), ypad[:, :, 1:L + 1], scal[:, 1:2], None, ALU.mult).then_inc(s_y_mix, 1)
                    dve.wait_ge(s_y_mix, ga + 1)
                    v.scalar_tensor_tensor(tiles(inp[:, :]), ypad[:, :, 0:L], scal[:, 2:3], tiles(ymix[:, :]),
                                           ALU.mult, ALU.add).then_inc(s_inp_sb, 1)
                if do_b:
                    dve.wait_ge(s_u_sb, gb + 1)
                    v.tensor_copy(U[:, 1:WRAP, :, 0:WRAP], U[:, 1:WRAP, :, H:UW]).then_inc(s_u_wrap, 1)
                    v.reduce_max(heads(mx[:, 0, :]), U[:, :, :, WRAP:UW].rearrange("p o k h -> p k h o"), AX)
                    dve.wait_ge(s_u_wrap, gb + 1)
                    v.reduce_max(heads(mx[:, 1, :]), shifted(1).rearrange("p o k h -> p k h o"), AX).then_inc(s_m_part, 1)
                    dve.wait_ge(s_m_part, gb + 1)
                    tt(mx[:, 2, :], mx[:, 0, :], mx[:, 1, :], ALU.max).then_inc(s_m_sb, 1)
                    dve.wait_ge(s_m_sb, gb + 1)
                    if due(gb):
                        dve.wait_ge(s_e_sb, gb)
                    m = heads(mx[:, 2, :]).unsqueeze(1)
                    tt(sc[:, 0:NO, :, :], U[:, :, :, WRAP:UW], m.to_broadcast([P, NO, G, H]), ALU.subtract)
                    tt(sc[:, NO:H, :, :][:, ::-1, :, :], shifted(1),
                       m.to_broadcast([P, H - NO, G, H]), ALU.subtract).then_inc(s_sc_sb, 1)
                if do_a:
                    dve.wait_ge(s_h_sb, ga + 1)
                    for k in range(G):
                        last = v.tensor_tensor_scan(stT[:, k * L:(k + 1) * L], decayt[:, :], hT[:, k * L:(k + 1) * L], 0.0,
                                                    ALU.mult, ALU.add)
                    last.then_inc(s_st_sb, 1)
                if do_c:
                    dve.wait_ge(s_lg_ps, gc + 1)
                    lg = ps_l[:, 0:G * NE].rearrange("p (k e) -> p k e", k=G)
                    v.reduce_max(lmax[:, :], lg, AX).then_inc(s_lmax_sb, 1)
                    dve.wait_ge(s_lmax_sb, gc + 1)
                    tt(ld[:, :, :], lg, lmax[:, :].unsqueeze(2).to_broadcast([P, G, NE]), ALU.subtract).then_inc(s_ld_sb, 1)
                    dve.wait_ge(s_ld_sb, gc + 1)
                    ts(hit[:, :, :], ld[:, :, :], 0.0, -float(2 * NE), ALU.is_equal, ALU.mult).then_inc(s_hit_sb, 1)
                    dve.wait_ge(s_hit_sb, gc + 1)
                    tt(score[:, :, :], hit[:, :, :], iota_e[:, :, :], ALU.add).then_inc(s_score_sb, 1)
                    dve.wait_ge(s_score_sb, gc + 1)
                    v.tensor_reduce(smin[:, :], score[:, :, :], AX, ALU.min).then_inc(s_smin_sb, 1)
                    dve.wait_ge(s_smin_sb, gc + 1)
                    tt(onehot[:, :, :], score[:, :, :], smin[:, :].unsqueeze(2).to_broadcast([P, G, NE]), ALU.is_equal).then_inc(s_oh_sb, 1)
                if do_b:
                    dve.wait_ge(s_e_sb, gb + 1)
                    v.reduce_sum(heads(esum[:, :]), e[:, :, :, :].rearrange("p o k h -> p k h o"), AX).then_inc(s_esum_sb, 1)
                    for c in range(H // KQ):
                        if c == 1:
                            dve.wait_ge(s_esum_sb, gb + 1)
                            v.reciprocal(rinv[:, :], esum[:, :]).then_inc(s_rinv_sb, 1)
                        if due(gb * (H // KQ) - (H // KQ - 1 - c)):
                            dve.wait_ge(s_av_ps, gb * (H // KQ) - (H // KQ - 1 - c))
                        ec = e[:, c * KQ:(c + 1) * KQ, :, :].rearrange("p o k h -> p (o k h)").unsqueeze(2).to_broadcast([P, KQ * G * H, D])
                        vo = bass.AP(tensor=kx, offset=c * KQ * D, ap=[[G * 2 * C, P], [D, KQ], [2 * C, G], [1, C]])
                        tt(av[c][:, :, :].rearrange("p o (kh d) -> p (o kh) d", d=D), ec, vo, ALU.mult).then_inc(s_av_sb, 1)
                        if c == 1 and do_a:
                            dve.wait_ge(s_o_ps, ga + 1)
                            v.scalar_tensor_tensor(x2T[:, :], ps_b[:, :], vec[:, 5:6], xT[:, :], ALU.add, ALU.add).then_inc(s_x2_sb, 1)
                elif do_a:
                    dve.wait_ge(s_o_ps, ga + 1)
                    v.scalar_tensor_tensor(x2T[:, :], ps_b[:, :], vec[:, 5:6], xT[:, :], ALU.add, ALU.add).then_inc(s_x2_sb, 1)
                if do_c:
                    dve.wait_ge(s_le_sb, gc + 1)
                    v.reduce_sum(lsum[:, :], le[:, :, :], AX).then_inc(s_lsum_sb, 1)
                    dve.wait_ge(s_rank_ps, gc + 1)
                    rk = ps_l[:, 64:64 + G * NE].rearrange("p (k e) -> p k e", k=G)
                    dve.wait_ge(s_base_sb, gc + 1)
                    tt(rank[:, :, :], rk, base[:, :].unsqueeze(1).to_broadcast([P, G, NE]), ALU.add).then_inc(s_rank_sb, 1)
                    dve.wait_ge(s_rank_sb, gc + 1)
                    tt(mine[:, :, :], rank[:, :, :], onehot[:, :, :], ALU.mult).then_inc(s_mine_sb, 1)
                    tt(base[:, :], base[:, :], ps_l[:, 128:128 + NE], ALU.add).then_inc(s_base_sb, 1)
                    dve.wait_ge(s_mine_sb, gc + 1)
                    v.reduce_sum(posf[:, :], mine[:, :, :], AX).then_inc(s_posf_sb, 1)
                    dve.wait_ge(s_lsum_sb, gc + 1)
                    dve.wait_ge(s_rows_free, gc + 1)
                    v.reciprocal(rows[u][:, :, CWT:CWT + 1], lsum[:, :].unsqueeze(2))
                    dve.wait_ge(s_posf_sb, gc + 1)
                    v.tensor_copy(pos[u][:, :], posf[:, :]).then_inc(s_pos_sb, 1)
            run_steps(dve, step)

            dve.wait_ge(s_base_sb, NG + 1)
            then(tt(cnt[:, :], base[:, :], ecap[:, :], ALU.subtract))
            then(tt(more[:, :, :], cnt[:, :].unsqueeze(2).to_broadcast([P, NE, B]), iota_k[:, :, :], ALU.is_gt))
            then(v.reduce_sum(ntile[:, :], more[:, :, :], AX))
            then(v.tensor_tensor_scan(cum[:, :], ones[:, 0:NE], ntile[:, :], 0.0, ALU.mult, ALU.add))
            then(tt(past[:, :, :], cum[:, :].unsqueeze(1).to_broadcast([P, NS, NE]), iota_i[:, :, :], ALU.is_le))
            tt(pastn[:, :, :], past[:, :, :], ntile[:, :].unsqueeze(1).to_broadcast([P, NS, NE]), ALU.mult)
            then(v.reduce_sum(tabf[:, 0, :], past[:, :, :], AX))
            then(v.reduce_sum(tabf[:, 1, :], pastn[:, :, :], AX))
            then(tt(tabf[:, 1, :], iota_i[:, :, 0], tabf[:, 1, :], ALU.subtract))
            then(ts(tabf[:, 2, :], tabf[:, 0, :], float(CAP), None, ALU.mult))
            then(v.scalar_tensor_tensor(tabf[:, 1, :], tabf[:, 1, :], float(P), tabf[:, 2, :], ALU.mult, ALU.add))
            then(ts(tabf[:, 1, :], tabf[:, 1, :], float(NE * CAP), None, ALU.min))
            then(ts(tabf[:, 0, :], tabf[:, 0, :], float(NE - 1), None, ALU.min))
            then(v.tensor_copy(tabf[:, 2, 0:NE], base[:, :]))
            v.tensor_copy(tab[:, :, :], tabf[:, :, :]).then_inc(s_tab_sb, 1)
            dve.wait_ge(s_tab_sb, 1)
            dve.wait_ge(s_exp_ld, 80)

            def bias_up(q, u):
                i = q * 3 + u
                r = dve.value_load(tab[0:1, 0, bass.ds(i, 1)], min_val=0, max_val=NE - 1)
                dve.wait_ge(s_h2_ps, i + 1)
                if due(i - 2):
                    dve.wait_ge(s_hg_sb, i - 2)
                tt(hb[u], ps_h[u][:, :], b1s[:, bass.ds(r, 1), :].rearrange("p a f -> p (a f)"), ALU.add).then_inc(s_hb_sb, 1)

            def turned(q, u):
                dve.wait_ge(s_hgT_ps, q * 3 + (u + 1))
                v.tensor_copy(hgT[u], ps_hT[u][:, :]).then_inc(s_hgT_sb, 1)

            def finish(q, u, first):
                i = q * 3 + u
                r = dve.value_load(tab[0:1, 0, bass.ds(i, 1)], min_val=0, max_val=NE - 1)
                dve.wait_ge(s_y2_ps, i + 1)
                tt(yb[u], ps_y[:, 0:C], b2s[:, bass.ds(r, 1), :].rearrange("p a f -> p (a f)"), ALU.add).then_inc(s_yb_sb, 1)
                if not first:
                    dve.wait_ge(o_out[u], q * 16)
                v.tensor_copy(oid[u][:, :], rt[u][:, CID:CID + 1]).then_inc(s_oid_sb, 1)
                dve.wait_ge(s_yb_sb, i + 1)
                v.scalar_tensor_tensor(orow[u], yb[u], rt[u][:, CWT:CWT + 1], rt[u][:, CX:CX + C],
                                       ALU.mult, ALU.add).then_inc(s_orow_sb, 1)

            bias_up(0, 0)
            bias_up(0, 1)
            turned(0, 0)
            bias_up(0, 2)
            turned(0, 1)
            finish(0, 0, True)

            def tile_step(q, u, first=False):
                bias_up(q, u)
                turned(*((q, u - 1) if u else (q - 1, 2)))
                finish(*((q, 0) if u == 2 else (q - 1, u + 1)), first)
            for u in range(3):
                tile_step(1, u, u < 2)
            with dve.Fori(2, NS // 3) as q:
                for u in range(3):
                    tile_step(q, u)
            q = NS // 3 - 1
            turned(q, 2)
            finish(q, 1, False)
            finish(q, 2, False)


_INS = ['x', 'cond_512', 'L0_cond_weight', 'L0_cond_bias', 'L0_cond_affine_w', 'L0_cond_affine_b', 'L0_attn_W_in',
        'L0_attn_b_in', 'L0_attn_W_out', 'L0_attn_b_out', 'L0_attn_decay', 'L0_attn_mix', 'L0_cond2_k_aff_w',
        'L0_cond2_k_aff_b', 'L0_cond2_k_w', 'L0_cond2_k_b', 'L0_cond2_o_aff_w', 'L0_cond2_o_aff_b', 'L0_cond2_o_w',
        'L0_cond2_o_b', 'L0_ffn_gate_w', 'L0_ffn_w1', 'L0_ffn_b1', 'L0_ffn_w2', 'L0_ffn_b2']


def kernel(**inputs):
    import numpy as np
    import concourse.bacc as bacc
    from concourse.bass_utils import run_bass_kernel_spmd

    nc = bacc.Bacc("TRN2", target_bir_lowering=False, num_devices=1)
    arrays, args = {}, []
    for name in _INS:
        a = np.ascontiguousarray(inputs[name])
        a = a.reshape(a.shape or (1,))
        arrays[f"in_{name}_dram"] = a
        args.append(nc.dram_tensor(f"in_{name}_dram", a.shape, mybir.dt.from_np(a.dtype), kind="ExternalInput").ap())
    shape = tuple(inputs['x'].shape)
    args.append(nc.dram_tensor("out_0_dram", shape, mybir.dt.float32, kind="ExternalOutput").ap())
    adaln_attn_ffn(nc, *args)
    r = run_bass_kernel_spmd(nc, [arrays], core_ids=[0])
    return r.results[0]["out_0_dram"]
```

```python
from contextlib import ExitStack

import concourse.bass as bass
from concourse import mybir

F32 = mybir.dt.float32
U32 = mybir.dt.uint32
ALU = mybir.AluOpType
ACT = mybir.ActivationFunctionType
AX = mybir.AxisListType.X

P = 128
CLAMP = 256.0
EPS = 1e-8


def adaln_attn_ffn(
    nc, x, cond, cw, c_bias, c_affw, c_affb, w_in, b_in, w_out, b_out, decay, mix,
    k_affw, k_affb, k_w, k_b, o_affw, o_affb, o_w, o_b, gate_w, w1, b1, w2, b2, out,
):
    B, L, C = x.shape
    WD = cond.shape[1]
    NE, _, F = w1.shape
    H, D = 16, C // 16
    assert L == P and C == P and D == 8
    G = 4
    GT = G * L
    NG = B // G
    NO = H // 2 + 1
    WRAP = H // 2
    UW = WRAP + H
    NLO = 4
    KQ = 4
    NCH = H // KQ
    FK = F // P
    T = B * L
    CAP = T + P
    NS = (T + NE * (P - 1)) // P
    RW = 2 * C + 2
    CZ, CX, CWT, CID = 0, C, 2 * C, 2 * C + 1
    SKIP = 2 * T

    xg = x.rearrange("(g k) t c -> g t k c", k=G)
    out_rows = out.rearrange("b t c -> (b t) c")
    rows_dram = nc.dram_tensor("expert_rows", (NE * CAP + P, RW), F32, kind="Internal").ap()

    with ExitStack() as ctx:
        def sb(name, shape, dt=F32):
            return ctx.enter_context(nc.sbuf_tensor(name, shape, dt))

        def sem(name):
            return ctx.enter_context(nc.semaphore(name))

        bank = [ctx.enter_context(nc.psum_tensor(f"bank{i}", [P, 512], F32)) for i in range(6)]
        ps_e = ctx.enter_context(nc.psum_tensor("ps_e", [P, H, G, H], F32))
        ps_a, ps_b, ps_av, ps_c, ps_d, ps_l = bank
        ps_h, ps_hT = bank[0:3], bank[3:6]
        pair = ps_e[:, :, :, :].rearrange("p o k h -> p (o k h)")
        ps_z, ps_y = pair[:, 0:P], pair[:, 512:512 + P]

        ident = sb("ident", [P, P])
        lower = sb("lower", [P, P])
        ones = sb("ones", [P, P])
        iota_e = sb("iota_e", [P, G, NE])
        ecap = sb("ecap", [P, NE])
        iota_k = sb("iota_k", [P, NE, B])
        iota_i = sb("iota_i", [P, NS, NE])
        tokid = sb("tokid", [P, B])
        tail = sb("tail", [P, RW])
        mats = sb("mats", [P, 5, P])
        matsT = sb("matsT", [P, 5, P])
        affs = sb("affs", [P, 3, WD])
        affsT = sb("affsT", [WD, 3, P])
        condt = sb("condt", [B, WD])
        condT = sb("condT", [WD, B])
        vec = sb("vec", [P, 8])
        scal = sb("scal", [P, 4])
        decayt = sb("decayt", [P, L])
        mods = sb("mods", [P, 3, 2, B])
        styles, demod = mods[:, :, 0, :], mods[:, :, 1, :]
        mod_a = [sb(f"mod_a{p}", [P, 2, 2, G]) for p in range(2)]
        mod_c = [sb(f"mod_c{p}", [P, 2, G]) for p in range(2)]
        styles2 = sb("styles2", [P, 3, B])
        sqT = sb("sqT", [P, 3, P])
        var = sb("var", [P, 3, B])
        root = sb("root", [P, 3, B])
        inv = sb("inv", [P, 3, B])
        newt = sb("newt", [P, 3, B])
        gatew = sb("gatew", [P, NE])
        w1s = sb("w1s", [P, NE, F])
        w2s = sb("w2s", [P, NE, FK, C])
        b1s = sb("b1s", [P, NE, F])
        b2s = sb("b2s", [P, NE, C])

        x_in = [sb(f"x_in{p}", [P, G, C]) for p in range(2)]
        xT = sb("xT", [P, GT])
        xm = sb("xm", [P, GT])
        yaff = sb("yaff", [P, GT])
        ypad = sb("ypad", [P, G, L + 1])
        ymix = sb("ymix", [P, GT])
        inp = sb("inp", [P, GT])
        hT = sb("hT", [P, GT])
        stT = sb("stT", [P, GT])
        x2T = sb("x2T", [P, GT])
        x2tok = sb("x2tok", [P, B, C])
        x2s = sb("x2s", [P, GT])
        kxT = sb("kxT", [P, GT])
        kext = [sb(f"kext{p}", [P, G, 2 * C]) for p in range(2)]
        qk = sb("qk", [P, NO, G, C])
        U = sb("U", [P, NO, G, UW])
        mx = sb("mx", [P, 3, G * H])
        sc = sb("sc", [P, H, G, H])
        e3 = sb("e3", [P, KQ, G, H])
        esum = sb("esum", [P, G * H])
        rinv = sb("rinv", [P, G * H])
        av = [sb(f"av{c}", [P, KQ, GT]) for c in range(H // KQ)]
        att = sb("att", [P, GT])
        attT = sb("attT", [P, GT])
        zT = sb("zT", [P, GT])
        rows = [sb(f"rows{p}", [P, G, RW]) for p in range(2)]
        lmax = sb("lmax", [P, G])
        ld = sb("ld", [P, G, NE])
        le = sb("le", [P, G, NE])
        lsum = sb("lsum", [P, G])
        hit = sb("hit", [P, G, NE])
        score = sb("score", [P, G, NE])
        smin = sb("smin", [P, G])
        onehot = sb("onehot", [P, G, NE])
        rank = sb("rank", [P, G, NE])
        mine = sb("mine", [P, G, NE])
        posf = sb("posf", [P, G])
        pos = [sb(f"pos{p}", [P, G], U32) for p in range(2)]
        base = sb("base", [P, NE])
        cnt = sb("cnt", [P, NE])
        more = sb("more", [P, NE, B])
        ntile = sb("ntile", [P, NE])
        cum = sb("cum", [P, NE])
        past = sb("past", [P, NS, NE])
        pastn = sb("pastn", [P, NS, NE])
        tabf = sb("tabf", [P, 3, NS])
        tab = sb("tab", [P, 3, NS], U32)
        zin = [sb(f"zin{u}", [P, C]) for u in range(3)]
        rest = [sb(f"rest{u}", [P, RW - C]) for u in range(3)]
        zt = [sb(f"zt{u}", [P, P]) for u in range(3)]
        hb, hg, hgT = ([qk[:, 3 * j + u, :, :].rearrange("p k c -> p (k c)") for u in range(3)] for j in range(3))
        yb = [inp[:, u * C:(u + 1) * C] for u in range(3)]
        orow = [x2s[:, u * C:(u + 1) * C] for u in range(3)]
        oid = [sb(f"oid{u}", [P, 1], U32) for u in range(3)]

        s_consts = sem("consts")
        s_selz = sem("selz")
        s_mats_ld = sem("mats_ld")
        s_aff_ld = sem("aff_ld")
        s_vec_ld = sem("vec_ld")
        s_scal_ld = sem("scal_ld")
        s_exp_ld = sem("exp_ld")
        s_setT_ps = sem("setT_ps")
        s_setT_sb = sem("setT_sb")
        s_aux_ps = sem("aux_ps")
        s_aux_sb = sem("aux_sb")
        s_sty_ps = sem("sty_ps")
        s_sty_sb = sem("sty_sb")
        s_sq_sb = sem("sq_sb")
        s_dem_ps = sem("dem_ps")
        s_var_sb = sem("var_sb")
        s_root_sb = sem("root_sb")
        s_dchain = sem("dchain")
        s_setup_done = sem("setup_done")
        s_xT_ps = sem("xT_ps")
        s_xT_sb = sem("xT_sb")
        s_xm_sb = sem("xm_sb")
        s_y_ps = sem("y_ps")
        s_y_aff = sem("y_aff")
        s_y_clip = sem("y_clip")
        s_y_mix = sem("y_mix")
        s_inp_sb = sem("inp_sb")
        s_h_ps = sem("h_ps")
        s_h_sb = sem("h_sb")
        s_st_sb = sem("st_sb")
        s_o_ps = sem("o_ps")
        s_x2_sb = sem("x2_sb")
        s_x2t_ps = sem("x2t_ps")
        s_x2tok_sb = sem("x2tok_sb")
        s_x2s_sb = sem("x2s_sb")
        s_kx_ps = sem("kx_ps")
        s_kxT_sb = sem("kxT_sb")
        s_kt_ps = sem("kt_ps")
        s_kext_sb = sem("kext_sb")
        s_qk_sb = sem("qk_sb")
        s_qkhi_sb = sem("qkhi_sb")
        s_ulo_sb = sem("ulo_sb")
        s_mod_a = sem("mod_a")
        s_mod_c = sem("mod_c")
        s_e3_sb = sem("e3_sb")
        s_av3_sb = sem("av3_sb")
        s_u_sb = sem("u_sb")
        s_u_wrap = sem("u_wrap")
        s_m_part = sem("m_part")
        s_m_sb = sem("m_sb")
        s_sc_sb = sem("sc_sb")
        s_e_sb = sem("e_sb")
        s_esum_sb = sem("esum_sb")
        s_rinv_sb = sem("rinv_sb")
        s_av_sb = sem("av_sb")
        s_av_ps = sem("av_ps")
        s_att_sb = sem("att_sb")
        s_at_ps = sem("at_ps")
        s_attT_sb = sem("attT_sb")
        s_z_ps = sem("z_ps")
        s_zT_sb = sem("zT_sb")
        s_zt_ps = sem("zt_ps")
        s_z_rows = sem("z_rows")
        s_lg_ps = sem("lg_ps")
        s_lmax_sb = sem("lmax_sb")
        s_ld_sb = sem("ld_sb")
        s_le_sb = sem("le_sb")
        s_lsum_sb = sem("lsum_sb")
        s_hit_sb = sem("hit_sb")
        s_score_sb = sem("score_sb")
        s_smin_sb = sem("smin_sb")
        s_oh_sb = sem("oh_sb")
        s_rank_ps = sem("rank_ps")
        s_rank_sb = sem("rank_sb")
        s_mine_sb = sem("mine_sb")
        s_posf_sb = sem("posf_sb")
        s_pos_sb = sem("pos_sb")
        s_rows_free = sem("rows_free")
        s_base_sb = sem("base_sb")
        s_x2_rows = sem("x2_rows")
        s_tab_sb = sem("tab_sb")
        s_tails_done = sem("tails_done")
        s_zero_done = sem("zero_done")
        s_zt2_ps = sem("zt2_ps")
        s_zt2_sb = sem("zt2_sb")
        s_h2_ps = sem("h2_ps")
        s_hb_sb = sem("hb_sb")
        s_hg_sb = sem("hg_sb")
        s_hgT_ps = sem("hgT_ps")
        s_hgT_sb = sem("hgT_sb")
        s_y2_ps = sem("y2_ps")
        s_yb_sb = sem("yb_sb")
        s_orow_sb = sem("orow_sb")
        s_oid_sb = sem("oid_sb")
        x_ld = [sem(f"x_ld{p}") for p in range(2)]
        scat = [sem(f"scat{p}") for p in range(2)]
        z_ld = [sem(f"z_ld{u}") for u in range(3)]
        rest_ld = [sem(f"rest_ld{u}") for u in range(3)]
        o_out = [sem(f"o_out{u}") for u in range(3)]

        def due(n):
            return not isinstance(n, int) or n > 0

        def tiles(ap):
            return ap.rearrange("p (k t) -> p k t", k=G)

        def per_batch(table):
            return table.unsqueeze(2).to_broadcast([P, G, L])

        def run_steps(eng, step):
            step(0, 0, True, False, False)
            step(1, 1, True, True, False)
            with eng.Fori(0, (NG - 2) // 2) as i:
                for u in range(2):
                    step(i * 2 + (2 + u), u, True, True, True)
            step(NG, 0, False, True, True)
            step(NG + 1, 1, False, False, True)

        block = ctx.enter_context(nc.Block())

        @block.sync
        def _(sp):
            for j, w in enumerate((cw, w_in, w_out, k_w, o_w)):
                sp.dma_start(mats[:, j, :], w).then_inc(s_mats_ld, 16)
            sp.dma_start(x_in[0][:, :, :], xg[0]).then_inc(x_ld[0], 16)
            sp.dma_start(x_in[1][:, :, :], xg[1]).then_inc(x_ld[1], 16)
            sp.dma_start(gatew[:, :], gate_w).then_inc(s_exp_ld, 16)
            sp.dma_start(w1s[:, :, :], w1.rearrange("e c f -> c e f")).then_inc(s_exp_ld, 16)
            sp.dma_start(w2s[:, :, :, :], w2.rearrange("e (k p) c -> p e k c", p=P)).then_inc(s_exp_ld, 16)
            sp.dma_start(b1s[:, :, :], b1.rearrange("(a e) f -> a e f", a=1).to_broadcast([P, NE, F])).then_inc(s_exp_ld, 16)
            sp.dma_start(b2s[:, :, :], b2.rearrange("(a e) f -> a e f", a=1).to_broadcast([P, NE, C])).then_inc(s_exp_ld, 16)
            with sp.Fori(0, (NG - 2) // 2) as i:
                for p in range(2):
                    sp.wait_ge(s_xT_ps, i * 2 + (1 + p))
                    sp.dma_start(x_in[p][:, :, :], xg[bass.ds(i * 2 + (2 + p), 1)].rearrange("a t k c -> (a t) k c")).then_inc(x_ld[p], 16)
            sp.wait_ge(s_consts, 1)
            sp.dma_start(rows_dram[NE * CAP:NE * CAP + P, :], tail[:, :]).then_inc(s_zero_done, 16)
            sp.wait_ge(s_tab_sb, 1)
            for ex in range(NE):
                r = sp.value_load(tab[0:1, 2, ex:ex + 1], min_val=ex * CAP, max_val=ex * CAP + T)
                sp.dma_start(rows_dram[bass.ds(r, P), :], tail[:, :]).then_inc(s_tails_done, 16)
            sp.wait_ge(s_zero_done, 16)
            sp.wait_ge(s_tails_done, 16 * NE)
            for p in range(2):
                sp.wait_ge(scat[p], 16 * G * (NG // 2))

            def load_z(q, u, first=False):
                i = q * 3 + u
                r = sp.value_load(tab[0:1, 1, bass.ds(i, 1)], min_val=0, max_val=NE * CAP)
                if not first:
                    sp.wait_ge(s_zt2_ps, i - 2)
                sp.dma_start(zin[u][:, :], rows_dram[bass.ds(r, P), CZ:CZ + C]).then_inc(z_ld[u], 16)

            def load_rest(q, u, first=False):
                i = q * 3 + u
                r = sp.value_load(tab[0:1, 1, bass.ds(i, 1)], min_val=0, max_val=NE * CAP)
                if not first:
                    sp.wait_ge(s_orow_sb, i - 2)
                sp.dma_start(rest[u][:, :], rows_dram[bass.ds(r, P), CX:RW]).then_inc(rest_ld[u], 16)
            for u in range(3):
                load_z(0, u, True)
            for u in range(3):
                load_rest(0, u, True)
            load_z(1, 0)
            load_z(1, 1)
            with sp.Fori(1, NS // 3 - 1) as q:
                for u in range(3):
                    load_z(*((q, 2) if u == 0 else (q + 1, u - 1)))
                    load_rest(q, u)
            q = NS // 3 - 1
            load_z(q, 2)
            for u in range(3):
                load_rest(q, u)

        @block.gpsimd
        def _(gp):
            gp.memset(tail[:, :], 0.0).then_inc(s_selz, 1)
            gp.memset(ident[:, :], 0.0).then_inc(s_selz, 1)
            gp.memset(ones[:, :], 1.0).then_inc(s_selz, 1)
            gp.wait_ge(s_selz, 3)
            gp.memset(tail[:, CID:CID + 1], float(SKIP))
            gp.affine_select(out=ident[:, :], in_=ident[:, :], compare_op=ALU.not_equal, fill=1.0, base=0,
                             pattern=[[-1, P]], channel_multiplier=1)
            gp.affine_select(out=lower[:, :], in_=ones[:, :], compare_op=ALU.is_gt, fill=0.0, base=0,
                             pattern=[[1, P]], channel_multiplier=-1)
            gp.iota(iota_e[:, :, :], pattern=[[0, G], [1, NE]], base=0, channel_multiplier=0, allow_small_or_imprecise_dtypes=True)
            gp.iota(ecap[:, :], pattern=[[CAP, NE]], base=0, channel_multiplier=0, allow_small_or_imprecise_dtypes=True)
            gp.iota(iota_k[:, :, :], pattern=[[0, NE], [P, B]], base=0, channel_multiplier=0, allow_small_or_imprecise_dtypes=True)
            gp.iota(iota_i[:, :, :], pattern=[[1, NS], [0, NE]], base=0, channel_multiplier=0, allow_small_or_imprecise_dtypes=True)
            gp.memset(ypad[:, :, 0:1], 0.0)
            gp.iota(tokid[:, :], pattern=[[L, B]], base=0, channel_multiplier=1, allow_small_or_imprecise_dtypes=True)
            gp.drain().then_inc(s_consts, 1)
            gp.sem_inc(s_rows_free, 2)
            gp.wait_ge(s_consts, 1)
            gp.wait_ge(s_setup_done, 1)

            def products(dst, o0, o1, kx):
                n = o1 - o0
                q = bass.AP(tensor=kx, offset=0, ap=[[G * 2 * C, P], [0, n], [2 * C, G], [1, C]])
                qo = bass.AP(tensor=kx, offset=o0 * D, ap=[[G * 2 * C, P], [D, n], [2 * C, G], [1, C]])
                return gp.tensor_tensor(dst, q, qo, ALU.mult)

            def step(s, u, do_a, do_b, do_c, do_d):
                ga, gb, gc, gd = s, s - 1, s - 2, s - 3
                if do_a:
                    gp.tensor_copy(mod_a[u][:, :, :, :], mods[:, 0:2, :, bass.ds(ga * G, G)]).then_inc(s_mod_a, 1)
                    gp.wait_ge(s_mod_a, ga + 1)
                    gp.wait_ge(s_xT_sb, ga + 1)
                    gp.tensor_tensor(tiles(xm[:, :]), tiles(xT[:, :]), per_batch(mod_a[u][:, 0, 0, :]), ALU.mult).then_inc(s_xm_sb, 1)
                if do_c:
                    gp.tensor_copy(mod_c[u][:, :, :], mods[:, 2, :, bass.ds(gc * G, G)]).then_inc(s_mod_c, 1)
                if do_d:
                    gp.wait_ge(s_x2_rows, gd + 1)
                    gp.wait_ge(s_z_rows, gd + 1)
                    gp.wait_ge(s_pos_sb, gd + 1)
                    gp.nop(nofuse=True)
                    for k in range(G):
                        gp.indirect_dma_start(rows_dram[:, :], bass.IndirectOffsetOnAxis(ap=pos[1 - u][:, k:k + 1], axis=0),
                                              rows[1 - u][:, k, :], None).then_inc(scat[1 - u], 16)
                if do_a:
                    gp.wait_ge(s_x2_sb, ga + 1)
                    gp.tensor_tensor(tiles(x2s[:, :]), tiles(x2T[:, :]), per_batch(mod_a[u][:, 1, 0, :]), ALU.mult).then_inc(s_x2s_sb, 1)
                if do_b:
                    c = NCH - 1
                    kx = kext[1 - u]
                    gp.wait_ge(s_e3_sb, gb + 1)
                    if due(gb * NCH):
                        gp.wait_ge(s_av_ps, gb * NCH)
                    ec = e3[:, :, :, :].rearrange("p o k h -> p (o k h)").unsqueeze(2).to_broadcast([P, KQ * G * H, D])
                    vo = bass.AP(tensor=kx, offset=c * KQ * D, ap=[[G * 2 * C, P], [D, KQ], [2 * C, G], [1, C]])
                    gp.tensor_tensor(av[c][:, :, :].rearrange("p o (kh d) -> p (o kh) d", d=D), ec, vo, ALU.mult).then_inc(s_av3_sb, 1)
                if do_d:
                    gp.wait_ge(scat[1 - u], (gd + u + 1) * (8 * G))
                    gp.nop(nofuse=True)
                    gp.sem_inc(s_rows_free, 1)
                if do_a:
                    gp.wait_ge(s_kext_sb, ga + 1)
                    if due(ga):
                        gp.wait_ge(s_u_sb, ga)
                    products(qk[:, NLO:NO, :, :], NLO, NO, kext[u]).then_inc(s_qkhi_sb, 1)
            step(0, 0, True, False, False, False)
            step(1, 1, True, True, False, False)
            step(2, 0, True, True, True, False)
            with gp.Fori(0, (NG - 4) // 2) as i:
                step(i * 2 + 3, 1, True, True, True, True)
                step(i * 2 + 4, 0, True, True, True, True)
            step(NG - 1, 1, True, True, True, True)
            step(NG, 0, False, True, True, True)
            step(NG + 1, 1, False, False, True, True)
            step(NG + 2, 0, False, False, False, True)

            def send(i, u, n):
                gp.wait_ge(s_orow_sb, i + 1)
                gp.wait_ge(s_oid_sb, i + 1)
                gp.nop(nofuse=True)
                gp.indirect_dma_start(out_rows, bass.IndirectOffsetOnAxis(ap=oid[u][:, 0:1], axis=0), orow[u], None,
                                      bounds_check=T - 1, oob_is_err=False).then_inc(o_out[u], 16)
            with gp.Fori(0, NS // 3) as i:
                for u in range(3):
                    send(i * 3 + u, u, i)
            for u in range(3):
                gp.wait_ge(o_out[u], 16 * (NS // 3))

        @block.tensor
        def _(pe):
            mm = nc.tensor.matmul

            def transpose4(dst, src):
                for k in range(G):
                    last = nc.tensor.transpose(dst[:, k * P:(k + 1) * P], src(k), ident[:, :])
                return last

            pe.wait_ge(s_consts, 1)
            pe.wait_ge(s_mats_ld, 80)
            transpose4(ps_a, lambda k: mats[:, k, :])
            nc.tensor.transpose(ps_b[:, 0:P], mats[:, 4, :], ident[:, :]).then_inc(s_setT_ps, 1)
            pe.wait_ge(s_aff_ld, 64)
            for j in range(3):
                nc.tensor.transpose(ps_av[0:WD, j * P:(j + 1) * P], affs[:, j, :], ident[:, :])
            nc.tensor.transpose(ps_c[0:WD, 0:B], condt[:, :], ident[0:B, 0:B]).then_inc(s_aux_ps, 1)
            pe.wait_ge(s_aux_sb, 1)
            for j in range(3):
                last = mm(ps_d[:, j * B:(j + 1) * B], affsT[:, j, :], condT[:, :], start=True, stop=True)
            last.then_inc(s_sty_ps, 1)
            pe.wait_ge(s_sq_sb, 1)
            for j in range(3):
                last = mm(ps_l[:, j * B:(j + 1) * B], sqT[:, j, :], styles2[:, j, :], start=True, stop=True)
            last.then_inc(s_dem_ps, 1)
            pe.wait_ge(s_setup_done, 1)
            pe.wait_ge(s_exp_ld, 80)

            def value_sums(g, c):
                if c == NCH - 1:
                    pe.wait_ge(s_av3_sb, g + 1)
                else:
                    pe.wait_ge(s_av_sb, g * (NCH - 1) + (c + 1))
                if c == 0 and due(g):
                    pe.wait_ge(s_att_sb, g)
                for o in range(KQ):
                    last = mm(ps_av[:, :], ident[:, :], av[c][:, o, :], start=c == 0 and o == 0, stop=c == NCH - 1 and o == KQ - 1)
                last.then_inc(s_av_ps, 1)

            def step(s, u, do_a, do_b, do_c):
                ga, gb, gc = s, s - 1, s - 2
                if do_a:
                    pe.wait_ge(x_ld[u], (s - u) * 8 + 16)
                    if due(ga):
                        pe.wait_ge(s_kext_sb, ga)
                    transpose4(ps_a, lambda k: x_in[u][:, k, :]).then_inc(s_xT_ps, 1)
                    pe.wait_ge(s_xm_sb, ga + 1)
                    mm(ps_b[:, :], matsT[:, 0, :], xm[:, :], start=True, stop=True).then_inc(s_y_ps, 1)
                if do_c:
                    pe.wait_ge(s_att_sb, gc + 1)
                    transpose4(ps_c, lambda k: att[:, k * P:(k + 1) * P]).then_inc(s_at_ps, 1)
                if do_a:
                    pe.wait_ge(s_inp_sb, ga + 1)
                    mm(ps_a[:, :], matsT[:, 1, :], inp[:, :], start=True, stop=True).then_inc(s_h_ps, 1)
                if do_c:
                    pe.wait_ge(s_attT_sb, gc + 1)
                    mm(ps_d[:, :], matsT[:, 4, :], attT[:, :], start=True, stop=True).then_inc(s_z_ps, 1)
                if do_a:
                    pe.wait_ge(s_st_sb, ga + 1)
                    mm(ps_b[:, :], matsT[:, 2, :], stT[:, :], start=True, stop=True).then_inc(s_o_ps, 1)
                if do_c:
                    pe.wait_ge(s_zT_sb, gc + 1)
                    for k in range(G):
                        last = mm(ps_l[:, k * NE:(k + 1) * NE], zT[:, k * P:(k + 1) * P], gatew[:, :], start=True, stop=True)
                    last.then_inc(s_lg_ps, 1)
                    transpose4(ps_c, lambda k: zT[:, k * P:(k + 1) * P]).then_inc(s_zt_ps, 1)
                if do_a:
                    pe.wait_ge(s_x2_sb, ga + 1)
                    transpose4(ps_a, lambda k: x2T[:, k * P:(k + 1) * P]).then_inc(s_x2t_ps, 1)
                    pe.wait_ge(s_x2s_sb, ga + 1)
                    mm(ps_b[:, :], matsT[:, 3, :], x2s[:, :], start=True, stop=True).then_inc(s_kx_ps, 1)
                if do_b:
                    value_sums(gb, 0)
                if do_a:
                    pe.wait_ge(s_kxT_sb, ga + 1)
                    transpose4(ps_a, lambda k: kxT[:, k * P:(k + 1) * P]).then_inc(s_kt_ps, 1)
                if do_c:
                    pe.wait_ge(s_oh_sb, gc + 1)
                    oh = onehot[:, :, :].rearrange("p k e -> p (k e)")
                    mm(ps_l[:, 64:64 + G * NE], lower[:, :], oh, start=True, stop=False)
                    for k in range(1, G):
                        mm(ps_l[:, 64 + k * NE:64 + G * NE], ones[:, :], oh[:, 0:(G - k) * NE], start=False, stop=k == G - 1)
                    for k in range(G):
                        last = mm(ps_l[:, 128:128 + NE], ones[:, :], onehot[:, k, :], start=k == 0, stop=k == G - 1)
                    last.then_inc(s_rank_ps, 1)
                if do_b:
                    value_sums(gb, 1)
                    value_sums(gb, 2)
                    value_sums(gb, 3)
            run_steps(pe, step)

            pe.wait_ge(s_tab_sb, 1)

            def z_transpose(q, u):
                pe.wait_ge(z_ld[u], q * 16 + 16)
                if due(q * 3 + u):
                    pe.wait_ge(s_zt2_sb, q * 3 + u)
                nc.tensor.transpose(ps_z, zin[u][:, :], ident[:, :]).then_inc(s_zt2_ps, 1)

            def up(q, u):
                i = q * 3 + u
                r = pe.value_load(tab[0:1, 0, bass.ds(i, 1)], min_val=0, max_val=NE - 1)
                pe.wait_ge(s_zt2_sb, i + 1)
                if due(i - 2):
                    pe.wait_ge(s_hb_sb, i - 2)
                mm(ps_h[u][:, :], zt[u][:, :], w1s[:, bass.ds(r, 1), :].rearrange("p a f -> p (a f)"),
                   start=True, stop=True).then_inc(s_h2_ps, 1)

            def turn(q, u):
                i = q * 3 + u
                pe.wait_ge(s_hg_sb, i + 1)
                transpose4(ps_hT[u], lambda k: hg[u][:, k * P:(k + 1) * P]).then_inc(s_hgT_ps, 1)

            def down(q, u):
                i = q * 3 + u
                r = pe.value_load(tab[0:1, 0, bass.ds(i, 1)], min_val=0, max_val=NE - 1)
                pe.wait_ge(s_hgT_sb, i + 1)
                if due(i):
                    pe.wait_ge(s_yb_sb, i)
                for k in range(FK):
                    last = mm(ps_y, hgT[u][:, k * P:(k + 1) * P],
                              w2s[:, bass.ds(r, 1), k, :].rearrange("p a c -> p (a c)"), start=k == 0, stop=k == FK - 1)
                last.then_inc(s_y2_ps, 1)

            def back(q, u, n):
                return (q, u - n) if u >= n else (q - 1, u - n + 3)

            z_transpose(0, 0)
            z_transpose(0, 1)
            for u in range(3):
                up(0, u)
                if u >= 1:
                    turn(0, u - 1)
                if u >= 2:
                    down(0, u - 2)
                z_transpose(*back(1, u, 1))
            with pe.Fori(1, NS // 3 - 1) as q:
                for u in range(3):
                    up(q, u)
                    turn(*back(q, u, 1))
                    down(*back(q, u, 2))
                    z_transpose(*back(q + 1, u, 1))
            q = NS // 3 - 1
            for u in range(3):
                up(q, u)
                turn(*back(q, u, 1))
                down(*back(q, u, 2))
                if u == 0:
                    z_transpose(q, 2)
            turn(q, 2)
            down(q, 1)
            down(q, 2)

        @block.scalar
        def _(act):
            a = nc.scalar.activation
            for j, v in enumerate((c_affw, k_affw, o_affw)):
                act.dma_start(affs[:, j, :], v).then_inc(s_aff_ld, 16)
            act.dma_start(condt[:, :], cond).then_inc(s_aff_ld, 16)
            for j, v in enumerate((c_affb, k_affb, o_affb, c_bias, b_in, b_out, k_b, o_b)):
                act.dma_start(vec[:, j:j + 1], v.rearrange("(p a) -> p a", a=1)).then_inc(s_vec_ld, 16)
            for j, v in enumerate((decay, mix)):
                act.dma_start(scal[:, j:j + 1], v.rearrange("(p a) -> p a", a=1).to_broadcast([P, 1])).then_inc(s_scal_ld, 16)
            act.wait_ge(s_setT_ps, 1)
            a(matsT[:, 0:4, :].rearrange("p j c -> p (j c)"), ps_a[:, :], ACT.Copy)
            a(matsT[:, 4, :], ps_b[:, 0:P], ACT.Copy).then_inc(s_setT_sb, 1)
            act.wait_ge(s_aux_ps, 1)
            a(condT[:, :], ps_c[0:WD, 0:B], ACT.Copy)
            a(affsT[:, :, :].rearrange("p j c -> p (j c)"), ps_av[0:WD, 0:3 * P], ACT.Copy).then_inc(s_aux_sb, 1)
            act.wait_ge(s_sty_ps, 1)
            act.wait_ge(s_vec_ld, 128)
            for j, gain in enumerate((float(WD) ** -0.5, 1.0, 1.0)):
                last = a(styles[:, j, :], ps_d[:, j * B:(j + 1) * B], ACT.Identity, bias=vec[:, j:j + 1], scale=gain)
            last.then_inc(s_sty_sb, 1)
            act.wait_ge(s_var_sb, 1)
            a(root[:, :, :], var[:, :, :], ACT.Sqrt).then_inc(s_root_sb, 1)
            act.wait_ge(s_setup_done, 1)

            def affine4(dst, src, scales, bias):
                for k in range(G):
                    last = a(dst[:, k * P:(k + 1) * P], src[:, k * P:(k + 1) * P], ACT.Identity,
                             scale=scales[:, k:k + 1], bias=bias)
                return last

            act.preload_act_table(ACT.Exp)

            def step(s, u, do_a, do_b, do_c):
                ga, gb, gc = s, s - 1, s - 2
                if do_a:
                    act.wait_ge(s_xT_ps, ga + 1)
                    a(xT[:, :], ps_a[:, :], ACT.Copy).then_inc(s_xT_sb, 1)
                    act.wait_ge(s_mod_a, ga + 1)
                    act.wait_ge(s_y_ps, ga + 1)
                    affine4(yaff, ps_b, mod_a[u][:, 0, 1, :], vec[:, 3:4]).then_inc(s_y_aff, 1)
                if do_c:
                    act.wait_ge(s_rows_free, gc + 1)
                    a(rows[u][:, :, CX:CX + C], x2tok[:, bass.ds(gc * G, G), :], ACT.Copy)
                    a(rows[u][:, :, CID:CID + 1], tokid[:, bass.ds(gc * G, G)].unsqueeze(2), ACT.Copy).then_inc(s_x2_rows, 1)
                if do_a:
                    act.wait_ge(s_y_clip, ga + 1)
                    a(tiles(ymix[:, :]), ypad[:, :, 1:L + 1], ACT.Copy, scale=scal[:, 1:2]).then_inc(s_y_mix, 1)
                if do_c:
                    act.wait_ge(s_mod_c, gc + 1)
                    act.wait_ge(s_at_ps, gc + 1)
                    affine4(attT, ps_c, mod_c[u][:, 0, :], 0.0).then_inc(s_attT_sb, 1)
                if do_a:
                    act.wait_ge(s_h_ps, ga + 1)
                    a(hT[:, :], ps_a[:, :], ACT.Relu, bias=vec[:, 4:5]).then_inc(s_h_sb, 1)
                if do_c:
                    act.wait_ge(s_z_ps, gc + 1)
                    affine4(zT, ps_d, mod_c[u][:, 1, :], vec[:, 7:8]).then_inc(s_zT_sb, 1)
                if do_b:
                    act.wait_ge(s_sc_sb, gb + 1)
                    a(ps_e[:, :, :, :], sc[:, :, :, :], ACT.Exp, scale=float(D) ** -0.5).then_inc(s_e_sb, 1)
                    a(e3[:, :, :, :], sc[:, H - KQ:H, :, :], ACT.Exp, scale=float(D) ** -0.5).then_inc(s_e3_sb, 1)
                if do_c:
                    act.wait_ge(s_zt_ps, gc + 1)
                    a(rows[u][:, :, CZ:CZ + C], tiles(ps_c[:, :]), ACT.Copy).then_inc(s_z_rows, 1)
                    act.wait_ge(s_ld_sb, gc + 1)
                    a(le[:, :, :], ld[:, :, :], ACT.Exp).then_inc(s_le_sb, 1)
                if do_a:
                    act.wait_ge(s_x2t_ps, ga + 1)
                    a(x2tok[:, bass.ds(ga * G, G), :], tiles(ps_a[:, :]), ACT.Copy).then_inc(s_x2tok_sb, 1)
                    act.wait_ge(s_kx_ps, ga + 1)
                    affine4(kxT, ps_b, mod_a[u][:, 1, 1, :], vec[:, 6:7]).then_inc(s_kxT_sb, 1)
                    act.wait_ge(s_kt_ps, ga + 1)
                    for r in range(2):
                        last = a(kext[u][:, :, r * C:(r + 1) * C], tiles(ps_a[:, :]), ACT.Copy)
                    last.then_inc(s_kext_sb, 1)
            run_steps(act, step)

            def z_copy(q, u):
                act.wait_ge(s_zt2_ps, q * 3 + (u + 1))
                a(zt[u][:, :], ps_z, ACT.Copy).then_inc(s_zt2_sb, 1)

            def gelu(q, u):
                act.wait_ge(s_hb_sb, q * 3 + (u + 1))
                a(hg[u], hb[u], ACT.Gelu).then_inc(s_hg_sb, 1)

            def turned(q, u):
                act.wait_ge(s_hgT_ps, q * 3 + (u + 1))
                a(hgT[u], ps_hT[u][:, :], ACT.Copy).then_inc(s_hgT_sb, 1)
            act.preload_act_table(ACT.Gelu)
            z_copy(0, 0)
            z_copy(0, 1)
            for u in range(3):
                if u >= 1:
                    turned(0, u - 1)
                gelu(0, u)
                z_copy(*((0, 2) if u == 0 else (1, u - 1)))
            with act.Fori(1, NS // 3 - 1) as q:
                for u in range(3):
                    turned(*((q, u - 1) if u else (q - 1, 2)))
                    gelu(q, u)
                    z_copy(*((q, 2) if u == 0 else (q + 1, u - 1)))
            q = NS // 3 - 1
            for u in range(3):
                turned(*((q, u - 1) if u else (q - 1, 2)))
                gelu(q, u)
                if u == 0:
                    z_copy(q, 2)
            turned(q, 2)

        @block.vector
        def _(dve):
            v = nc.vector
            tt, ts = v.tensor_tensor, v.tensor_scalar

            chain = [0]

            def then(ins):
                chain[0] += 1
                ins.then_inc(s_dchain, 1)
                dve.wait_ge(s_dchain, chain[0])

            dve.wait_ge(s_consts, 1)
            v.tensor_copy(base[:, :], ecap[:, :]).then_inc(s_base_sb, 1)
            dve.wait_ge(s_scal_ld, 32)
            then(ts(decayt[:, :], ones[:, :], scal[:, 0:1], None, ALU.mult))
            then(ts(scal[:, 2:3], scal[:, 1:2], -1.0, 1.0, ALU.mult, ALU.add))
            dve.wait_ge(s_setT_sb, 1)
            dve.wait_ge(s_sty_sb, 1)
            tt(styles2[:, :, :], styles, styles, ALU.mult)
            tt(sqT[:, 0, :], matsT[:, 0, :], matsT[:, 0, :], ALU.mult)
            tt(sqT[:, 1:3, :], matsT[:, 3:5, :], matsT[:, 3:5, :], ALU.mult).then_inc(s_sq_sb, 1)
            dve.wait_ge(s_dem_ps, 1)
            ts(var[:, :, :].rearrange("p j b -> p (j b)"), ps_l[:, 0:3 * B], EPS, None, ALU.add).then_inc(s_var_sb, 1)
            dve.wait_ge(s_root_sb, 1)
            then(v.reciprocal(inv[:, :, :], root[:, :, :]))
            then(tt(newt[:, :, :], inv[:, :, :], inv[:, :, :], ALU.mult))
            then(tt(newt[:, :, :], newt[:, :, :], var[:, :, :], ALU.mult))
            then(ts(newt[:, :, :], newt[:, :, :], -0.5, 1.5, ALU.mult, ALU.add))
            tt(demod, inv[:, :, :], newt[:, :, :], ALU.mult).then_inc(s_setup_done, 1)

            def shifted(o1):
                return bass.AP(tensor=U, offset=o1 * G * UW + WRAP - o1,
                               ap=[[NO * G * UW, P], [G * UW - 1, H - NO], [UW, G], [1, H]])

            def heads(ap):
                return ap.rearrange("p (k h) -> p k h", k=G)

            def step(s, u, do_a, do_b, do_c):
                ga, gb, gc = s, s - 1, s - 2
                kx = kext[1 - u]
                if do_b:
                    dve.wait_ge(s_kext_sb, gb + 1)
                    q = bass.AP(tensor=kx, offset=0, ap=[[G * 2 * C, P], [0, NLO], [2 * C, G], [1, C]])
                    qo = bass.AP(tensor=kx, offset=0, ap=[[G * 2 * C, P], [D, NLO], [2 * C, G], [1, C]])
                    tt(qk[:, 0:NLO, :, :], q, qo, ALU.mult).then_inc(s_qk_sb, 1)
                    dve.wait_ge(s_qk_sb, gb + 1)
                    v.reduce_sum(U[:, 0:NLO, :, WRAP:UW], qk[:, 0:NLO, :, :].rearrange("p o k (h d) -> p (o k) h d", d=D), AX).then_inc(s_ulo_sb, 1)
                if do_a:
                    dve.wait_ge(s_y_aff, ga + 1)
                    ts(ypad[:, :, 1:L + 1], tiles(yaff[:, :]), CLAMP, -CLAMP, ALU.min, ALU.max).then_inc(s_y_clip, 1)
                if do_c:
                    dve.wait_ge(s_av_ps, (gc + 1) * NCH)
                    dve.wait_ge(s_rinv_sb, gc + 1)
                    tt(att[:, :].rearrange("p (h d) -> p h d", d=D), ps_av[:, :].rearrange("p (h d) -> p h d", d=D),
                       rinv[:, :].unsqueeze(2).to_broadcast([P, G * H, D]), ALU.mult).then_inc(s_att_sb, 1)
                if do_b:
                    dve.wait_ge(s_qkhi_sb, gb + 1)
                    v.reduce_sum(U[:, NLO:NO, :, WRAP:UW], qk[:, NLO:NO, :, :].rearrange("p o k (h d) -> p (o k) h d", d=D), AX).then_inc(s_u_sb, 1)
                if do_a:
                    dve.wait_ge(s_y_mix, ga + 1)
                    v.scalar_tensor_tensor(tiles(inp[:, :]), ypad[:, :, 0:L], scal[:, 2:3], tiles(ymix[:, :]),
                                           ALU.mult, ALU.add).then_inc(s_inp_sb, 1)
                if do_b:
                    dve.wait_ge(s_u_sb, gb + 1)
                    v.tensor_copy(U[:, 1:WRAP, :, 0:WRAP], U[:, 1:WRAP, :, H:UW]).then_inc(s_u_wrap, 1)
                    v.reduce_max(heads(mx[:, 0, :]), U[:, :, :, WRAP:UW].rearrange("p o k h -> p k h o"), AX)
                    dve.wait_ge(s_u_wrap, gb + 1)
                    v.reduce_max(heads(mx[:, 1, :]), shifted(1).rearrange("p o k h -> p k h o"), AX).then_inc(s_m_part, 1)
                    dve.wait_ge(s_m_part, gb + 1)
                    tt(mx[:, 2, :], mx[:, 0, :], mx[:, 1, :], ALU.max).then_inc(s_m_sb, 1)
                if do_a:
                    dve.wait_ge(s_h_sb, ga + 1)
                    for k in range(G):
                        last = v.tensor_tensor_scan(stT[:, k * L:(k + 1) * L], decayt[:, :], hT[:, k * L:(k + 1) * L], 0.0,
                                                    ALU.mult, ALU.add)
                    last.then_inc(s_st_sb, 1)
                if do_b:
                    dve.wait_ge(s_m_sb, gb + 1)
                    if due(gb):
                        dve.wait_ge(s_e3_sb, gb)
                    m = heads(mx[:, 2, :]).unsqueeze(1)
                    tt(sc[:, 0:NO, :, :], U[:, :, :, WRAP:UW], m.to_broadcast([P, NO, G, H]), ALU.subtract)
                    tt(sc[:, NO:H, :, :][:, ::-1, :, :], shifted(1), m.to_broadcast([P, H - NO, G, H]), ALU.subtract).then_inc(s_sc_sb, 1)
                if do_a:
                    dve.wait_ge(s_o_ps, ga + 1)
                    v.scalar_tensor_tensor(x2T[:, :], ps_b[:, :], vec[:, 5:6], xT[:, :], ALU.add, ALU.add).then_inc(s_x2_sb, 1)

                def value_products(c):
                    if due(gb * NCH - (NCH - 1 - c)):
                        dve.wait_ge(s_av_ps, gb * NCH - (NCH - 1 - c))
                    ec = ps_e[:, c * KQ:(c + 1) * KQ, :, :].rearrange("p o k h -> p (o k h)").unsqueeze(2).to_broadcast([P, KQ * G * H, D])
                    vo = bass.AP(tensor=kx, offset=c * KQ * D, ap=[[G * 2 * C, P], [D, KQ], [2 * C, G], [1, C]])
                    tt(av[c][:, :, :].rearrange("p o (kh d) -> p (o kh) d", d=D), ec, vo, ALU.mult).then_inc(s_av_sb, 1)
                if do_b:
                    dve.wait_ge(s_e_sb, gb + 1)
                    value_products(0)
                    v.reduce_sum(heads(esum[:, :]), ps_e[:, :, :, :].rearrange("p o k h -> p k h o"), AX).then_inc(s_esum_sb, 1)
                if do_c:
                    dve.wait_ge(s_lg_ps, gc + 1)
                    lg = ps_l[:, 0:G * NE].rearrange("p (k e) -> p k e", k=G)
                    v.reduce_max(lmax[:, :], lg, AX).then_inc(s_lmax_sb, 1)
                    dve.wait_ge(s_lmax_sb, gc + 1)
                    tt(ld[:, :, :], lg, lmax[:, :].unsqueeze(2).to_broadcast([P, G, NE]), ALU.subtract).then_inc(s_ld_sb, 1)
                    dve.wait_ge(s_ld_sb, gc + 1)
                    ts(hit[:, :, :], ld[:, :, :], 0.0, -float(2 * NE), ALU.is_equal, ALU.mult).then_inc(s_hit_sb, 1)
                    dve.wait_ge(s_hit_sb, gc + 1)
                    tt(score[:, :, :], hit[:, :, :], iota_e[:, :, :], ALU.add).then_inc(s_score_sb, 1)
                    dve.wait_ge(s_score_sb, gc + 1)
                    v.tensor_reduce(smin[:, :], score[:, :, :], AX, ALU.min).then_inc(s_smin_sb, 1)
                    dve.wait_ge(s_smin_sb, gc + 1)
                    tt(onehot[:, :, :], score[:, :, :], smin[:, :].unsqueeze(2).to_broadcast([P, G, NE]), ALU.is_equal).then_inc(s_oh_sb, 1)
                if do_b:
                    value_products(1)
                    dve.wait_ge(s_esum_sb, gb + 1)
                    v.reciprocal(rinv[:, :], esum[:, :]).then_inc(s_rinv_sb, 1)
                    value_products(2)
                if do_c:
                    dve.wait_ge(s_le_sb, gc + 1)
                    v.reduce_sum(lsum[:, :], le[:, :, :], AX).then_inc(s_lsum_sb, 1)
                    dve.wait_ge(s_rank_ps, gc + 1)
                    rk = ps_l[:, 64:64 + G * NE].rearrange("p (k e) -> p k e", k=G)
                    dve.wait_ge(s_base_sb, gc + 1)
                    tt(rank[:, :, :], rk, base[:, :].unsqueeze(1).to_broadcast([P, G, NE]), ALU.add).then_inc(s_rank_sb, 1)
                    dve.wait_ge(s_rank_sb, gc + 1)
                    tt(mine[:, :, :], rank[:, :, :], onehot[:, :, :], ALU.mult).then_inc(s_mine_sb, 1)
                    tt(base[:, :], base[:, :], ps_l[:, 128:128 + NE], ALU.add).then_inc(s_base_sb, 1)
                    dve.wait_ge(s_mine_sb, gc + 1)
                    v.reduce_sum(posf[:, :], mine[:, :, :], AX).then_inc(s_posf_sb, 1)
                    dve.wait_ge(s_lsum_sb, gc + 1)
                    dve.wait_ge(s_rows_free, gc + 1)
                    v.reciprocal(rows[u][:, :, CWT:CWT + 1], lsum[:, :].unsqueeze(2))
                    dve.wait_ge(s_posf_sb, gc + 1)
                    v.tensor_copy(pos[u][:, :], posf[:, :]).then_inc(s_pos_sb, 1)
            run_steps(dve, step)

            dve.wait_ge(s_base_sb, NG + 1)
            then(tt(cnt[:, :], base[:, :], ecap[:, :], ALU.subtract))
            then(tt(more[:, :, :], cnt[:, :].unsqueeze(2).to_broadcast([P, NE, B]), iota_k[:, :, :], ALU.is_gt))
            then(v.reduce_sum(ntile[:, :], more[:, :, :], AX))
            then(v.tensor_tensor_scan(cum[:, :], ones[:, 0:NE], ntile[:, :], 0.0, ALU.mult, ALU.add))
            then(tt(past[:, :, :], cum[:, :].unsqueeze(1).to_broadcast([P, NS, NE]), iota_i[:, :, :], ALU.is_le))
            tt(pastn[:, :, :], past[:, :, :], ntile[:, :].unsqueeze(1).to_broadcast([P, NS, NE]), ALU.mult)
            then(v.reduce_sum(tabf[:, 0, :], past[:, :, :], AX))
            then(v.reduce_sum(tabf[:, 1, :], pastn[:, :, :], AX))
            then(tt(tabf[:, 1, :], iota_i[:, :, 0], tabf[:, 1, :], ALU.subtract))
            then(ts(tabf[:, 2, :], tabf[:, 0, :], float(CAP), None, ALU.mult))
            then(v.scalar_tensor_tensor(tabf[:, 1, :], tabf[:, 1, :], float(P), tabf[:, 2, :], ALU.mult, ALU.add))
            then(ts(tabf[:, 1, :], tabf[:, 1, :], float(NE * CAP), None, ALU.min))
            then(ts(tabf[:, 0, :], tabf[:, 0, :], float(NE - 1), None, ALU.min))
            then(v.tensor_copy(tabf[:, 2, 0:NE], base[:, :]))
            v.tensor_copy(tab[:, :, :], tabf[:, :, :]).then_inc(s_tab_sb, 1)
            dve.wait_ge(s_tab_sb, 1)
            dve.wait_ge(s_exp_ld, 80)

            def bias_up(q, u):
                i = q * 3 + u
                r = dve.value_load(tab[0:1, 0, bass.ds(i, 1)], min_val=0, max_val=NE - 1)
                dve.wait_ge(s_h2_ps, i + 1)
                if due(i - 2):
                    dve.wait_ge(s_hg_sb, i - 2)
                tt(hb[u], ps_h[u][:, :], b1s[:, bass.ds(r, 1), :].rearrange("p a f -> p (a f)"), ALU.add).then_inc(s_hb_sb, 1)

            def finish(q, u, first):
                i = q * 3 + u
                r = dve.value_load(tab[0:1, 0, bass.ds(i, 1)], min_val=0, max_val=NE - 1)
                dve.wait_ge(s_y2_ps, i + 1)
                tt(yb[u], ps_y, b2s[:, bass.ds(r, 1), :].rearrange("p a f -> p (a f)"), ALU.add).then_inc(s_yb_sb, 1)
                if not first:
                    dve.wait_ge(o_out[u], q * 16)
                dve.wait_ge(rest_ld[u], q * 16 + 16)
                v.tensor_copy(oid[u][:, :], rest[u][:, CID - C:CID - C + 1]).then_inc(s_oid_sb, 1)
                dve.wait_ge(s_yb_sb, i + 1)
                v.scalar_tensor_tensor(orow[u], yb[u], rest[u][:, CWT - C:CWT - C + 1], rest[u][:, 0:C],
                                       ALU.mult, ALU.add).then_inc(s_orow_sb, 1)

            for u in range(3):
                bias_up(0, u)
            finish(0, 0, True)

            def tile_step(q, u, first=False):
                bias_up(q, u)
                finish(*((q, 0) if u == 2 else (q - 1, u + 1)), first)
            for u in range(3):
                tile_step(1, u, u < 2)
            with dve.Fori(2, NS // 3) as q:
                for u in range(3):
                    tile_step(q, u)
            q = NS // 3 - 1
            finish(q, 1, False)
            finish(q, 2, False)


_INS = ['x', 'cond_512', 'L0_cond_weight', 'L0_cond_bias', 'L0_cond_affine_w', 'L0_cond_affine_b', 'L0_attn_W_in',
        'L0_attn_b_in', 'L0_attn_W_out', 'L0_attn_b_out', 'L0_attn_decay', 'L0_attn_mix', 'L0_cond2_k_aff_w',
        'L0_cond2_k_aff_b', 'L0_cond2_k_w', 'L0_cond2_k_b', 'L0_cond2_o_aff_w', 'L0_cond2_o_aff_b', 'L0_cond2_o_w',
        'L0_cond2_o_b', 'L0_ffn_gate_w', 'L0_ffn_w1', 'L0_ffn_b1', 'L0_ffn_w2', 'L0_ffn_b2']


def kernel(**inputs):
    import numpy as np
    import concourse.bacc as bacc
    from concourse.bass_utils import run_bass_kernel_spmd

    nc = bacc.Bacc("TRN2", target_bir_lowering=False, num_devices=1)
    arrays, args = {}, []
    for name in _INS:
        a = np.ascontiguousarray(inputs[name])
        a = a.reshape(a.shape or (1,))
        arrays[f"in_{name}_dram"] = a
        args.append(nc.dram_tensor(f"in_{name}_dram", a.shape, mybir.dt.from_np(a.dtype), kind="ExternalInput").ap())
    shape = tuple(inputs['x'].shape)
    args.append(nc.dram_tensor("out_0_dram", shape, mybir.dt.float32, kind="ExternalOutput").ap())
    adaln_attn_ffn(nc, *args)
    r = run_bass_kernel_spmd(nc, [arrays], core_ids=[0])
    return r.results[0]["out_0_dram"]
```

```python
from contextlib import ExitStack

import concourse.bass as bass
from concourse import mybir

F32 = mybir.dt.float32
U32 = mybir.dt.uint32
ALU = mybir.AluOpType
ACT = mybir.ActivationFunctionType
AX = mybir.AxisListType.X

P = 128
CLAMP = 256.0
EPS = 1e-8


def adaln_attn_ffn(
    nc, x, cond, cw, c_bias, c_affw, c_affb, w_in, b_in, w_out, b_out, decay, mix,
    k_affw, k_affb, k_w, k_b, o_affw, o_affb, o_w, o_b, gate_w, w1, b1, w2, b2, out,
):
    B, L, C = x.shape
    WD = cond.shape[1]
    NE, _, F = w1.shape
    H, D = 16, C // 16
    assert L == P and C == P and D == 8
    G = 4
    GT = G * L
    NG = B // G
    NO = H // 2 + 1
    WRAP = H // 2
    UW = WRAP + H
    NLO = 2
    KQ = 4
    NCH = H // KQ
    FK = F // P
    T = B * L
    CAP = T + P
    NS = (T + NE * (P - 1)) // P
    RW = 2 * C + 2
    CZ, CX, CWT, CID = 0, C, 2 * C, 2 * C + 1
    SKIP = 2 * T

    xg = x.rearrange("(g k) t c -> g t k c", k=G)
    out_rows = out.rearrange("b t c -> (b t) c")
    rows_dram = nc.dram_tensor("expert_rows", (NE * CAP + P, RW), F32, kind="Internal").ap()

    with ExitStack() as ctx:
        def sb(name, shape, dt=F32):
            return ctx.enter_context(nc.sbuf_tensor(name, shape, dt))

        def sem(name):
            return ctx.enter_context(nc.semaphore(name))

        bank = [ctx.enter_context(nc.psum_tensor(f"bank{i}", [P, 512], F32)) for i in range(6)]
        ps_e = ctx.enter_context(nc.psum_tensor("ps_e", [P, H, G, H], F32))
        ps_a, ps_b, ps_av, ps_c, ps_d, ps_l = bank
        ps_h, ps_y = bank[0:3], [bank[3 + u][:, 0:P] for u in range(3)]
        ps_z = ps_e[:, :, :, :].rearrange("p o k h -> p (o k h)")[:, 0:P]

        ident = sb("ident", [P, P])
        lower = sb("lower", [P, P])
        ones = sb("ones", [P, P])
        iota_e = sb("iota_e", [P, G, NE])
        ecap = sb("ecap", [P, NE])
        iota_k = sb("iota_k", [P, NE, B])
        iota_i = sb("iota_i", [P, NS, NE])
        tokid = sb("tokid", [P, B])
        tail = sb("tail", [P, RW])
        mats = sb("mats", [P, 5, P])
        matsT = sb("matsT", [P, 5, P])
        affs = sb("affs", [P, 3, WD])
        affsT = sb("affsT", [WD, 3, P])
        condt = sb("condt", [B, WD])
        condT = sb("condT", [WD, B])
        vec = sb("vec", [P, 8])
        scal = sb("scal", [P, 4])
        decayt = sb("decayt", [P, L])
        mods = sb("mods", [P, 3, 2, B])
        styles, demod = mods[:, :, 0, :], mods[:, :, 1, :]
        mod_a = [sb(f"mod_a{p}", [P, 2, 2, G]) for p in range(2)]
        mod_c = [sb(f"mod_c{p}", [P, 2, G]) for p in range(2)]
        styles2 = sb("styles2", [P, 3, B])
        sqT = sb("sqT", [P, 3, P])
        var = sb("var", [P, 3, B])
        root = sb("root", [P, 3, B])
        inv = sb("inv", [P, 3, B])
        newt = sb("newt", [P, 3, B])
        gatew = sb("gatew", [P, NE])
        w1s = sb("w1s", [P, NE, F])
        w2s = sb("w2s", [P, NE, FK, C])
        b1rows = sb("b1rows", [NE * FK, P])
        b1s = sb("b1s", [P, NE, FK])
        w1t = [sb(f"w1t{u}", [P, F]) for u in range(3)]
        b2s = sb("b2s", [P, NE, C])
        b1t = [sb(f"b1t{u}", [P, FK]) for u in range(3)]
        b2t = [sb(f"b2t{u}", [P, C]) for u in range(3)]

        x_in = [sb(f"x_in{p}", [P, G, C]) for p in range(2)]
        xm = sb("xm", [P, GT])
        yaff = sb("yaff", [P, GT])
        ypad = sb("ypad", [P, G, L + 1])
        ymix = sb("ymix", [P, GT])
        inp = sb("inp", [P, GT])
        hT = sb("hT", [P, GT])
        stT = sb("stT", [P, GT])
        x2T = sb("x2T", [P, GT])
        x2tok = sb("x2tok", [P, B, C])
        x2s = sb("x2s", [P, GT])
        kxT = sb("kxT", [P, GT])
        kext = [sb(f"kext{p}", [P, G, 2 * C]) for p in range(2)]
        qk = sb("qk", [P, NO, G, C])
        U = sb("U", [P, NO, G, UW])
        mx = sb("mx", [P, 3, G * H])
        sc = sb("sc", [P, H, G, H])
        e3 = sb("e3", [P, KQ, G, H])
        esum = sb("esum", [P, G * H])
        rinv = sb("rinv", [P, G * H])
        av = [sb(f"av{c}", [P, KQ, GT]) for c in range(H // KQ)]
        att = sb("att", [P, GT])
        attT = sb("attT", [P, GT])
        zT = sb("zT", [P, GT])
        rows = [sb(f"rows{p}", [P, G, RW]) for p in range(2)]
        lmax = sb("lmax", [P, G])
        ld = sb("ld", [P, G, NE])
        le = sb("le", [P, G, NE])
        lsum = sb("lsum", [P, G])
        hit = sb("hit", [P, G, NE])
        score = sb("score", [P, G, NE])
        smin = sb("smin", [P, G])
        onehot = sb("onehot", [P, G + 1, NE])
        rank = sb("rank", [P, G, NE])
        mine = sb("mine", [P, G, NE])
        posf = sb("posf", [P, G])
        pos = [sb(f"pos{p}", [P, G], U32) for p in range(2)]
        base = sb("base", [P, NE])
        cnt = sb("cnt", [P, NE])
        more = sb("more", [P, NE, B])
        ntile = sb("ntile", [P, NE])
        cum = sb("cum", [P, NE])
        past = sb("past", [P, NS, NE])
        pastn = sb("pastn", [P, NS, NE])
        tabf = sb("tabf", [P, 3, NS])
        tab = sb("tab", [P, 2, NS], U32)
        tail_row = sb("tail_row", [P, NE], U32)
        zin = [sb(f"zin{u}", [P, C]) for u in range(3)]
        rest = [sb(f"rest{u}", [P, RW - C]) for u in range(3)]
        zt = [sb(f"zt{u}", [P, P]) for u in range(3)]
        hb, hg = ([qk[:, 3 * j + u, :, :].rearrange("p k c -> p (k c)") for u in range(3)] for j in range(2))
        yb = [inp[:, u * C:(u + 1) * C] for u in range(3)]
        orow = [x2s[:, u * C:(u + 1) * C] for u in range(3)]
        oid = [sb(f"oid{u}", [P, 1], U32) for u in range(3)]

        s_consts = sem("consts")
        s_selz = sem("selz")
        s_mats_ld = sem("mats_ld")
        s_aff_ld = sem("aff_ld")
        s_vec_ld = sem("vec_ld")
        s_scal_ld = sem("scal_ld")
        s_gate_ld = sem("gate_ld")
        s_exp_ld = sem("exp_ld")
        s_setT_ps = sem("setT_ps")
        s_setT_sb = sem("setT_sb")
        s_aux_ps = sem("aux_ps")
        s_aux_sb = sem("aux_sb")
        s_sty_ps = sem("sty_ps")
        s_sty_sb = sem("sty_sb")
        s_sq_sb = sem("sq_sb")
        s_dem_ps = sem("dem_ps")
        s_var_sb = sem("var_sb")
        s_root_sb = sem("root_sb")
        s_dchain = sem("dchain")
        s_setup_done = sem("setup_done")
        s_xT_ps = sem("xT_ps")
        s_xm_sb = sem("xm_sb")
        s_y_ps = sem("y_ps")
        s_y_aff = sem("y_aff")
        s_y_clip = sem("y_clip")
        s_y_mix = sem("y_mix")
        s_inp_sb = sem("inp_sb")
        s_h_ps = sem("h_ps")
        s_h_sb = sem("h_sb")
        s_st_sb = sem("st_sb")
        s_o_ps = sem("o_ps")
        s_x2_sb = sem("x2_sb")
        s_x2t_ps = sem("x2t_ps")
        s_x2s_sb = sem("x2s_sb")
        s_kx_ps = sem("kx_ps")
        s_kxT_sb = sem("kxT_sb")
        s_kt_ps = sem("kt_ps")
        s_kext_sb = sem("kext_sb")
        s_qk_sb = sem("qk_sb")
        s_qkhi_sb = sem("qkhi_sb")
        s_mod_a = sem("mod_a")
        s_mod_c = sem("mod_c")
        s_e3_sb = sem("e3_sb")
        s_av3_prod = sem("av3_prod")
        s_av3_half = sem("av3_half")
        s_av3_sb = sem("av3_sb")
        s_u_sb = sem("u_sb")
        s_u_wrap = sem("u_wrap")
        s_m_part = sem("m_part")
        s_m_sb = sem("m_sb")
        s_sclo_sb = sem("sclo_sb")
        s_sc_sb = sem("sc_sb")
        s_elo_sb = sem("elo_sb")
        s_e_sb = sem("e_sb")
        s_esum_sb = sem("esum_sb")
        s_rinv_sb = sem("rinv_sb")
        s_av_sb = sem("av_sb")
        s_av_ps = sem("av_ps")
        s_att_sb = sem("att_sb")
        s_at_ps = sem("at_ps")
        s_attT_sb = sem("attT_sb")
        s_z_ps = sem("z_ps")
        s_zT_sb = sem("zT_sb")
        s_zt_ps = sem("zt_ps")
        s_z_rows = sem("z_rows")
        s_lg_ps = sem("lg_ps")
        s_lmax_sb = sem("lmax_sb")
        s_ld_sb = sem("ld_sb")
        s_le_sb = sem("le_sb")
        s_lsum_sb = sem("lsum_sb")
        s_hit_sb = sem("hit_sb")
        s_score_sb = sem("score_sb")
        s_smin_sb = sem("smin_sb")
        s_oh_sb = sem("oh_sb")
        s_rank_ps = sem("rank_ps")
        s_rank_sb = sem("rank_sb")
        s_mine_sb = sem("mine_sb")
        s_posf_sb = sem("posf_sb")
        s_pos_sb = sem("pos_sb")
        s_rows_free = sem("rows_free")
        s_base_sb = sem("base_sb")
        s_x2_rows = sem("x2_rows")
        s_tab_sb = sem("tab_sb")
        s_tail_row = sem("tail_row")
        s_tails_done = sem("tails_done")
        s_zero_done = sem("zero_done")
        s_b1_ps = sem("b1_ps")
        s_b1_sb = sem("b1_sb")
        s_zt2_ps = sem("zt2_ps")
        s_zt2_sb = [sem(f"zt2_sb{u}") for u in range(3)]
        s_h2_ps = sem("h2_ps")
        s_hb_sb = sem("hb_sb")
        s_hg_sb = [sem(f"hg_sb{u}") for u in range(3)]
        s_y2_ps = sem("y2_ps")
        s_yb_sb = sem("yb_sb")
        s_orow_sb = sem("orow_sb")
        s_oid_sb = sem("oid_sb")
        x_ld = [sem(f"x_ld{p}") for p in range(2)]
        scat = [sem(f"scat{p}") for p in range(2)]
        z_ld = [sem(f"z_ld{u}") for u in range(3)]
        rest_ld = [sem(f"rest_ld{u}") for u in range(3)]
        o_out = [sem(f"o_out{u}") for u in range(3)]

        def due(n):
            return not isinstance(n, int) or n > 0

        def tiles(ap):
            return ap.rearrange("p (k t) -> p k t", k=G)

        def per_batch(table):
            return table.unsqueeze(2).to_broadcast([P, G, L])

        def table_entry(kind, i, engine, most):
            return nc.values_load(tab[0:1, kind, bass.ds(i, 1)], engines=(engine,), min_val=0, max_val=most,
                                  skip_runtime_bounds_check_because="the table was cut off at its largest entries")

        def tail_of(ex, engine):
            return nc.values_load(tail_row[0:1, ex:ex + 1], engines=(engine,), min_val=ex * CAP, max_val=ex * CAP + T,
                                  skip_runtime_bounds_check_because="an expert has no more rows than there are tokens")

        def run_steps(eng, step):
            step(0, 0, True, True, False, False, False)
            step(1, 1, True, True, True, False, False)
            step(2, 0, True, True, True, True, False)
            with eng.Fori(0, (NG - 4) // 2) as i:
                step(i * 2 + 3, 1, True, True, True, True, True)
                step(i * 2 + 4, 0, True, True, True, True, True)
            step(NG - 1, 1, False, True, True, True, True)
            step(NG, 0, False, False, True, True, True)
            step(NG + 1, 1, False, False, False, True, True)
            step(NG + 2, 0, False, False, False, False, True)

        block = ctx.enter_context(nc.Block())

        @block.sync
        def _(sp):
            for j, w in enumerate((cw, w_in, w_out, k_w, o_w)):
                sp.dma_start(mats[:, j, :], w).then_inc(s_mats_ld, 16)
            for j, v in enumerate((c_affb, k_affb, o_affb, c_bias, b_in, b_out, k_b, o_b)):
                sp.dma_start(vec[:, j:j + 1], v.rearrange("(p a) -> p a", a=1)).then_inc(s_vec_ld, 16)
            sp.dma_start(x_in[1][:, :, :], xg[1]).then_inc(x_ld[1], 16)
            sp.dma_start(gatew[:, :], gate_w).then_inc(s_gate_ld, 16)
            sp.wait_ge(s_vec_ld, 128)
            sp.wait_ge(s_scal_ld, 32)
            sp.wait_ge(x_ld[1], 16)
            sp.dma_start(w1s[:, :, :], w1.rearrange("e c f -> c e f")).then_inc(s_exp_ld, 16)
            sp.dma_start(w2s[:, :, :, :], w2.rearrange("e (k p) c -> p e k c", p=P)).then_inc(s_exp_ld, 16)
            sp.dma_start(b1rows[:, :], b1.rearrange("e (k p) -> (e k) p", p=P)).then_inc(s_exp_ld, 16)
            sp.dma_start(b2s[:, :, :], b2.rearrange("(a e) f -> a e f", a=1).to_broadcast([P, NE, C])).then_inc(s_exp_ld, 16)

            def load_x(g, i, p):
                sp.wait_ge(s_o_ps, i * 2 + (1 + p))
                sp.dma_start(x_in[p][:, :, :], xg[bass.ds(g, 1)].rearrange("a t k c -> (a t) k c")).then_inc(x_ld[p], 16)

            def free_rows(i, p):
                sp.wait_ge(scat[p], i * (16 * G) + 16 * G)
                sp.nop(nofuse=True)
                sp.sem_inc(s_rows_free, 1)

            with sp.Fori(0, 2) as i:
                for p in range(2):
                    load_x(i * 2 + (2 + p), i, p)
            with sp.Fori(2, (NG - 2) // 2) as i:
                for p in range(2):
                    load_x(i * 2 + (2 + p), i, p)
                    free_rows(i - 2, p)
            with sp.Fori((NG - 2) // 2 - 2, (NG - 2) // 2) as i:
                for p in range(2):
                    free_rows(i, p)
            sp.wait_ge(s_consts, 1)
            sp.dma_start(rows_dram[NE * CAP:NE * CAP + P, :], tail[:, :]).then_inc(s_zero_done, 16)
            sp.wait_ge(s_tail_row, 1)
            for ex in range(0, NE, 2):
                r = tail_of(ex, mybir.EngineType.SP)
                sp.dma_start(rows_dram[bass.ds(r, P), :], tail[:, :]).then_inc(s_tails_done, 16)
            sp.wait_ge(s_tab_sb, 1)
            sp.wait_ge(s_zero_done, 16)
            sp.wait_ge(s_tails_done, 16 * NE)
            for p in range(2):
                sp.wait_ge(scat[p], 16 * G * (NG // 2))

            def first_row(q, u):
                return table_entry(1, q * 3 + u, mybir.EngineType.SP, NE * CAP)

            def load_z(q, u, r, first=False):
                if not first:
                    sp.wait_ge(s_zt2_ps, q * 3 + (u - 2))
                sp.dma_start(zin[u][:, :], rows_dram[bass.ds(r, P), CZ:CZ + C]).then_inc(z_ld[u], 16)

            def load_rest(q, u, r, first=False):
                if not first:
                    sp.wait_ge(s_orow_sb, q * 3 + (u - 2))
                sp.dma_start(rest[u][:, :], rows_dram[bass.ds(r, P), CX:RW]).then_inc(rest_ld[u], 16)

            r = [first_row(0, u) for u in range(3)]
            for u in range(3):
                load_z(0, u, r[u], True)
            for u in range(3):
                load_rest(0, u, r[u], True)
            load_z(1, 0, first_row(1, 0))
            load_z(1, 1, first_row(1, 1))
            with sp.Fori(1, NS // 3 - 1) as q:
                r2 = first_row(q, 2)
                load_z(q, 2, r2)
                load_rest(q, 0, first_row(q, 0))
                load_z(q + 1, 0, first_row(q + 1, 0))
                load_rest(q, 1, first_row(q, 1))
                load_z(q + 1, 1, first_row(q + 1, 1))
                load_rest(q, 2, r2)
            q = NS // 3 - 1
            load_z(q, 2, first_row(q, 2))
            for u in range(3):
                load_rest(q, u, first_row(q, u))

        @block.gpsimd
        def _(gp):
            gp.memset(tail[:, :], 0.0).then_inc(s_selz, 1)
            gp.memset(ident[:, :], 0.0).then_inc(s_selz, 1)
            gp.memset(ones[:, :], 1.0).then_inc(s_selz, 1)
            gp.wait_ge(s_selz, 3)
            gp.memset(tail[:, CID:CID + 1], float(SKIP))
            gp.affine_select(out=ident[:, :], in_=ident[:, :], compare_op=ALU.not_equal, fill=1.0, base=0,
                             pattern=[[-1, P]], channel_multiplier=1)
            gp.affine_select(out=lower[:, :], in_=ones[:, :], compare_op=ALU.is_gt, fill=0.0, base=0,
                             pattern=[[1, P]], channel_multiplier=-1)
            gp.iota(iota_e[:, :, :], pattern=[[0, G], [1, NE]], base=0, channel_multiplier=0, allow_small_or_imprecise_dtypes=True)
            gp.iota(ecap[:, :], pattern=[[CAP, NE]], base=0, channel_multiplier=0, allow_small_or_imprecise_dtypes=True)
            gp.iota(iota_k[:, :, :], pattern=[[0, NE], [P, B]], base=0, channel_multiplier=0, allow_small_or_imprecise_dtypes=True)
            gp.iota(iota_i[:, :, :], pattern=[[1, NS], [0, NE]], base=0, channel_multiplier=0, allow_small_or_imprecise_dtypes=True)
            gp.memset(ypad[:, :, 0:1], 0.0)
            gp.memset(onehot[:, G:G + 1, :], 0.0)
            gp.iota(tokid[:, :], pattern=[[L, B]], base=0, channel_multiplier=1, allow_small_or_imprecise_dtypes=True)
            gp.drain().then_inc(s_consts, 1)
            gp.sem_inc(s_rows_free, 2)
            gp.wait_ge(s_consts, 1)
            gp.wait_ge(s_setup_done, 1)

            def products(dst, o0, o1, kx):
                n = o1 - o0
                q = bass.AP(tensor=kx, offset=0, ap=[[G * 2 * C, P], [0, n], [2 * C, G], [1, C]])
                qo = bass.AP(tensor=kx, offset=o0 * D, ap=[[G * 2 * C, P], [D, n], [2 * C, G], [1, C]])
                return gp.tensor_tensor(dst, q, qo, ALU.mult)

            def modulations(g, u):
                gp.tensor_copy(mod_a[u][:, :, :, :], mods[:, 0:2, :, bass.ds(g * G, G)]).then_inc(s_mod_a, 1)

            modulations(0, 0)

            def step(s, u, do_h, do_a, do_b, do_c, do_d):
                ga, gb, gc, gd = s, s - 1, s - 2, s - 3
                if do_h:
                    modulations(s + 1, 1 - u)
                if do_c:
                    gp.tensor_copy(mod_c[u][:, :, :], mods[:, 2, :, bass.ds(gc * G, G)]).then_inc(s_mod_c, 1)
                if do_a:
                    gp.wait_ge(s_mod_a, ga + 1)
                    gp.wait_ge(s_x2_sb, ga + 1)
                    gp.tensor_tensor(tiles(x2s[:, :]), tiles(x2T[:, :]), per_batch(mod_a[u][:, 1, 0, :]), ALU.mult).then_inc(s_x2s_sb, 1)
                if do_b:
                    c = NCH - 1
                    kx = kext[1 - u]
                    gp.wait_ge(s_e3_sb, gb + 1)
                    if due(gb * NCH - 1):
                        gp.wait_ge(s_av_ps, gb * NCH - 1)
                    ec = e3[:, :, :, :].rearrange("p o k h -> p (o k h)").unsqueeze(2).to_broadcast([P, KQ * G * H, D])
                    vo = bass.AP(tensor=kx, offset=c * KQ * D, ap=[[G * 2 * C, P], [D, KQ], [2 * C, G], [1, C]])
                    gp.tensor_tensor(av[c][:, :, :].rearrange("p o (kh d) -> p (o kh) d", d=D), ec, vo, ALU.mult).then_inc(s_av3_prod, 1)
                if do_a:
                    gp.wait_ge(s_kext_sb, ga + 1)
                    if due(ga):
                        gp.wait_ge(s_u_sb, ga)
                    products(qk[:, NLO:NO, :, :], NLO, NO, kext[u]).then_inc(s_qkhi_sb, 1)
                if do_b:
                    a3 = av[NCH - 1]
                    gp.wait_ge(s_av3_prod, gb + 1)
                    gp.tensor_tensor(a3[:, 0:2, :], a3[:, 0:2, :], a3[:, 2:4, :], ALU.add).then_inc(s_av3_half, 1)
                    gp.wait_ge(s_av3_half, gb + 1)
                    gp.tensor_tensor(a3[:, 0, :], a3[:, 0, :], a3[:, 1, :], ALU.add).then_inc(s_av3_sb, 1)
                if do_d:
                    gp.wait_ge(s_x2_rows, gd + 1)
                    gp.wait_ge(s_z_rows, gd + 1)
                    gp.wait_ge(s_pos_sb, gd + 1)
                    gp.nop(nofuse=True)
                    for k in range(G):
                        gp.indirect_dma_start(rows_dram[:, :], bass.IndirectOffsetOnAxis(ap=pos[1 - u][:, k:k + 1], axis=0),
                                              rows[1 - u][:, k, :], None).then_inc(scat[1 - u], 16)
            run_steps(gp, step)

            def send(i, u, n):
                gp.wait_ge(s_orow_sb, i + 1)
                gp.wait_ge(s_oid_sb, i + 1)
                gp.nop(nofuse=True)
                gp.indirect_dma_start(out_rows, bass.IndirectOffsetOnAxis(ap=oid[u][:, 0:1], axis=0), orow[u], None,
                                      bounds_check=T - 1, oob_is_err=False).then_inc(o_out[u], 16)
            with gp.Fori(0, NS // 3) as i:
                for u in range(3):
                    send(i * 3 + u, u, i)
            for u in range(3):
                gp.wait_ge(o_out[u], 16 * (NS // 3))

        @block.tensor
        def _(pe):
            mm = nc.tensor.matmul

            def transpose4(dst, src):
                for k in range(G):
                    last = nc.tensor.transpose(dst[:, k * P:(k + 1) * P], src(k), ident[:, :])
                return last

            pe.wait_ge(s_consts, 1)
            pe.wait_ge(s_mats_ld, 80)
            transpose4(ps_a, lambda k: mats[:, k, :])
            nc.tensor.transpose(ps_b[:, 0:P], mats[:, 4, :], ident[:, :]).then_inc(s_setT_ps, 1)
            pe.wait_ge(s_aff_ld, 64)
            for j in range(3):
                nc.tensor.transpose(ps_av[0:WD, j * P:(j + 1) * P], affs[:, j, :], ident[:, :])
            nc.tensor.transpose(ps_c[0:WD, 0:B], condt[:, :], ident[0:B, 0:B]).then_inc(s_aux_ps, 1)
            pe.wait_ge(x_ld[0], 16)
            transpose4(ps_d, lambda k: x_in[0][:, k, :]).then_inc(s_xT_ps, 1)
            pe.wait_ge(s_aux_sb, 1)
            for j in range(3):
                last = mm(ps_c[:, P + j * B:P + (j + 1) * B], affsT[:, j, :], condT[:, :], start=True, stop=True)
            last.then_inc(s_sty_ps, 1)
            pe.wait_ge(s_sq_sb, 1)
            for j in range(3):
                last = mm(ps_l[:, j * B:(j + 1) * B], sqT[:, j, :], styles2[:, j, :], start=True, stop=True)
            last.then_inc(s_dem_ps, 1)
            pe.wait_ge(s_gate_ld, 16)

            def value_sums(g, c, offsets=range(KQ)):
                if c == NCH - 1:
                    pe.wait_ge(s_av3_sb, g + 1)
                else:
                    pe.wait_ge(s_av_sb, g * (NCH - 1) + (c + 1))
                if c == 0 and due(g):
                    pe.wait_ge(s_att_sb, g)
                if c == NCH - 1:
                    offsets = [0]
                for o in offsets:
                    last = mm(ps_av[:, :], ident[:, :], av[c][:, o, :], start=c == 0 and o == 0, stop=c == NCH - 2 and o == KQ - 1)
                if c == NCH - 1 or o == KQ - 1:
                    last.then_inc(s_av_ps, 1)

            def head_turn(g, u):
                pe.wait_ge(x_ld[u], (g - u) * 8 + 16)
                transpose4(ps_d, lambda k: x_in[u][:, k, :]).then_inc(s_xT_ps, 1)

            def head_product(g):
                pe.wait_ge(s_xm_sb, g + 1)
                mm(ps_b[:, :], matsT[:, 0, :], xm[:, :], start=True, stop=True).then_inc(s_y_ps, 1)

            def head_hidden(g):
                pe.wait_ge(s_inp_sb, g + 1)
                if due(g):
                    pe.wait_ge(s_kext_sb, g)
                mm(ps_a[:, :], matsT[:, 1, :], inp[:, :], start=True, stop=True).then_inc(s_h_ps, 1)

            head_product(0)
            head_hidden(0)

            def step(s, u, do_h, do_a, do_b, do_c, do_d):
                ga, gb, gc, gd = s, s - 1, s - 2, s - 3
                if do_c:
                    value_sums(gc, 2, range(0, 1))
                    value_sums(gc, 3)
                if do_a:
                    for k in range(G):
                        mm(ps_b[:, k * P:(k + 1) * P], x_in[u][:, k, :], ident[:, :], start=k == 0, stop=False)
                    pe.wait_ge(s_st_sb, ga + 1)
                    mm(ps_b[:, :], matsT[:, 2, :], stT[:, :], start=False, stop=True).then_inc(s_o_ps, 1)
                if do_c:
                    value_sums(gc, 2, range(1, KQ // 2))
                if do_a:
                    pe.wait_ge(s_x2_sb, ga + 1)
                    transpose4(ps_a, lambda k: x2T[:, k * P:(k + 1) * P]).then_inc(s_x2t_ps, 1)
                if do_h:
                    head_turn(s + 1, 1 - u)
                if do_a:
                    pe.wait_ge(s_x2s_sb, ga + 1)
                    mm(ps_b[:, :], matsT[:, 3, :], x2s[:, :], start=True, stop=True).then_inc(s_kx_ps, 1)
                if do_c:
                    value_sums(gc, 2, range(KQ // 2, KQ))
                if do_a:
                    pe.wait_ge(s_kxT_sb, ga + 1)
                    transpose4(ps_a, lambda k: kxT[:, k * P:(k + 1) * P]).then_inc(s_kt_ps, 1)
                if do_d:
                    pe.wait_ge(s_oh_sb, gd + 1)
                    oh = onehot[:, :, :].rearrange("p k e -> p (k e)")
                    mm(ps_l[:, 64:64 + (G + 1) * NE], lower[:, :], oh, start=True, stop=False)
                    for k in range(1, G + 1):
                        last = mm(ps_l[:, 64 + k * NE:64 + (G + 1) * NE], ones[:, :], oh[:, 0:(G + 1 - k) * NE], start=False, stop=k == G)
                    last.then_inc(s_rank_ps, 1)
                if do_h:
                    head_product(s + 1)
                if do_c:
                    pe.wait_ge(s_att_sb, gc + 1)
                    if due(gc):
                        pe.wait_ge(s_z_rows, gc)
                    transpose4(ps_c, lambda k: att[:, k * P:(k + 1) * P]).then_inc(s_at_ps, 1)
                if do_b:
                    value_sums(gb, 0)
                if do_c:
                    pe.wait_ge(s_attT_sb, gc + 1)
                    mm(ps_d[:, :], matsT[:, 4, :], attT[:, :], start=True, stop=True).then_inc(s_z_ps, 1)
                if do_b:
                    value_sums(gb, 1)
                if do_c:
                    pe.wait_ge(s_zT_sb, gc + 1)
                    if due(gc):
                        pe.wait_ge(s_base_sb, gc + 1)
                    for k in range(G):
                        last = mm(ps_l[:, k * NE:(k + 1) * NE], zT[:, k * P:(k + 1) * P], gatew[:, :], start=True, stop=True)
                    last.then_inc(s_lg_ps, 1)
                    transpose4(ps_c, lambda k: zT[:, k * P:(k + 1) * P]).then_inc(s_zt_ps, 1)
                if do_h:
                    head_hidden(s + 1)
            run_steps(pe, step)

            pe.wait_ge(s_tab_sb, 1)
            pe.wait_ge(s_exp_ld, 64)
            nc.tensor.transpose(ps_h[0][:, 0:NE * FK], b1rows[:, :], ident[0:NE * FK, 0:NE * FK]).then_inc(s_b1_ps, 1)

            def expert(q, u):
                return table_entry(0, q * 3 + u, mybir.EngineType.PE, NE - 1)

            def z_transpose(q, u):
                pe.wait_ge(z_ld[u], q * 16 + 16)
                nc.tensor.transpose(ps_z, zin[u][:, :], ident[:, :]).then_inc(s_zt2_ps, 1)

            def up(q, u):
                pe.wait_ge(s_zt2_sb[u], q + 1)
                for k in range(FK):
                    last = mm(ps_h[u][:, k * P:(k + 1) * P], w1t[u][:, k * P:(k + 1) * P], zt[u][:, :], start=True, stop=True)
                last.then_inc(s_h2_ps, 1)

            def down(q, u, r):
                pe.wait_ge(s_hg_sb[u], q + 1)
                for k in range(FK):
                    last = mm(ps_y[u], hg[u][:, k * P:(k + 1) * P],
                              w2s[:, bass.ds(r, 1), k, :].rearrange("p a c -> p (a c)"), start=k == 0, stop=k == FK - 1)
                last.then_inc(s_y2_ps, 1)

            z_transpose(0, 0)
            up(0, 0)
            z_transpose(0, 1)
            up(0, 1)
            z_transpose(0, 2)
            down(0, 0, expert(0, 0))
            up(0, 2)
            z_transpose(1, 0)
            down(0, 1, expert(0, 1))

            def tile_steps(q, feed=3):
                for u in range(3):
                    before = (q, u - 1) if u else (q - 1, 2)
                    up(q, u)
                    r = expert(*before)
                    if u < feed:
                        z_transpose(*((q, u + 1) if u < 2 else (q + 1, 0)))
                    down(*before, r)
            with pe.Fori(1, NS // 3 - 1) as q:
                tile_steps(q)
            q = NS // 3 - 1
            tile_steps(q, feed=2)
            down(q, 2, expert(q, 2))

        @block.scalar
        def _(act):
            a = nc.scalar.activation
            for j, v in enumerate((c_affw, k_affw, o_affw)):
                act.dma_start(affs[:, j, :], v).then_inc(s_aff_ld, 16)
            act.dma_start(condt[:, :], cond).then_inc(s_aff_ld, 16)
            for j, v in enumerate((decay, mix)):
                act.dma_start(scal[:, j:j + 1], v.rearrange("(p a) -> p a", a=1).to_broadcast([P, 1])).then_inc(s_scal_ld, 16)
            act.dma_start(x_in[0][:, :, :], xg[0]).then_inc(x_ld[0], 16)
            act.preload_act_table(ACT.Sqrt)
            def affine4(dst, src, scales, bias):
                for k in range(G):
                    last = a(dst[:, k * P:(k + 1) * P], src[:, k * P:(k + 1) * P], ACT.Identity,
                             scale=scales[:, k:k + 1], bias=bias)
                return last

            def head_style(g, scales):
                act.wait_ge(s_xT_ps, g + 1)
                affine4(xm, ps_d, scales, 0.0).then_inc(s_xm_sb, 1)

            act.wait_ge(s_setT_ps, 1)
            a(matsT[:, 0:4, :].rearrange("p j c -> p (j c)"), ps_a[:, :], ACT.Copy)
            a(matsT[:, 4, :], ps_b[:, 0:P], ACT.Copy).then_inc(s_setT_sb, 1)
            act.wait_ge(s_aux_ps, 1)
            a(condT[:, :], ps_c[0:WD, 0:B], ACT.Copy)
            a(affsT[:, :, :].rearrange("p j c -> p (j c)"), ps_av[0:WD, 0:3 * P], ACT.Copy).then_inc(s_aux_sb, 1)
            act.wait_ge(s_sty_ps, 1)
            act.wait_ge(s_vec_ld, 128)
            for j, gain in enumerate((float(WD) ** -0.5, 1.0, 1.0)):
                last = a(styles[:, j, :], ps_c[:, P + j * B:P + (j + 1) * B], ACT.Identity, bias=vec[:, j:j + 1], scale=gain)
            last.then_inc(s_sty_sb, 1)
            act.wait_ge(s_sty_sb, 1)
            head_style(0, styles[:, 0, 0:G])
            act.wait_ge(s_var_sb, 1)
            a(root[:, :, :], var[:, :, :], ACT.Sqrt).then_inc(s_root_sb, 1)

            act.preload_act_table(ACT.Exp)
            act.wait_ge(s_setup_done, 1)

            def head_demod(g, scales):
                act.wait_ge(s_y_ps, g + 1)
                affine4(yaff, ps_b, scales, vec[:, 3:4]).then_inc(s_y_aff, 1)

            head_demod(0, demod[:, 0, 0:G])

            def step(s, u, do_h, do_a, do_b, do_c, do_d):
                ga, gb, gc, gd = s, s - 1, s - 2, s - 3
                if do_a:
                    act.wait_ge(s_y_clip, ga + 1)
                    a(tiles(ymix[:, :]), ypad[:, :, 1:L + 1], ACT.Copy, scale=scal[:, 1:2]).then_inc(s_y_mix, 1)
                    act.wait_ge(s_h_ps, ga + 1)
                    a(hT[:, :], ps_a[:, :], ACT.Relu, bias=vec[:, 4:5]).then_inc(s_h_sb, 1)
                if do_d:
                    act.wait_ge(s_zt_ps, gd + 1)
                    a(rows[1 - u][:, :, CZ:CZ + C], tiles(ps_c[:, :]), ACT.Copy).then_inc(s_z_rows, 1)
                if do_a:
                    act.wait_ge(s_o_ps, ga + 1)
                    a(x2T[:, :], ps_b[:, :], ACT.Identity, bias=vec[:, 5:6]).then_inc(s_x2_sb, 1)
                if do_b:
                    act.wait_ge(s_sclo_sb, gb + 1)
                    a(ps_e[:, 0:H // 2, :, :], sc[:, 0:H // 2, :, :], ACT.Exp, scale=float(D) ** -0.5).then_inc(s_elo_sb, 1)
                    act.wait_ge(s_sc_sb, gb + 1)
                    a(ps_e[:, H // 2:H, :, :], sc[:, H // 2:H, :, :], ACT.Exp, scale=float(D) ** -0.5).then_inc(s_e_sb, 1)
                    a(e3[:, :, :, :], sc[:, H - KQ:H, :, :], ACT.Exp, scale=float(D) ** -0.5).then_inc(s_e3_sb, 1)
                if do_a:
                    act.wait_ge(s_x2t_ps, ga + 1)
                    a(x2tok[:, bass.ds(ga * G, G), :], tiles(ps_a[:, :]), ACT.Copy)
                if do_a:
                    act.wait_ge(s_kx_ps, ga + 1)
                    affine4(kxT, ps_b, mod_a[u][:, 1, 1, :], vec[:, 6:7]).then_inc(s_kxT_sb, 1)
                if do_d:
                    act.wait_ge(s_ld_sb, gd + 1)
                    a(le[:, :, :], ld[:, :, :], ACT.Exp).then_inc(s_le_sb, 1)
                if do_h:
                    act.wait_ge(s_mod_a, s + 2)
                    head_style(s + 1, mod_a[1 - u][:, 0, 0, :])
                if do_a:
                    act.wait_ge(s_kt_ps, ga + 1)
                    for r in range(2):
                        last = a(kext[u][:, :, r * C:(r + 1) * C], tiles(ps_a[:, :]), ACT.Copy)
                    last.then_inc(s_kext_sb, 1)
                if do_h:
                    head_demod(s + 1, mod_a[1 - u][:, 0, 1, :])
                if do_c:
                    act.wait_ge(s_mod_c, gc + 1)
                    act.wait_ge(s_at_ps, gc + 1)
                    affine4(attT, ps_c, mod_c[u][:, 0, :], 0.0).then_inc(s_attT_sb, 1)
                    act.wait_ge(s_rows_free, gc + 1)
                    a(rows[u][:, :, CX:CX + C], x2tok[:, bass.ds(gc * G, G), :], ACT.Copy)
                    a(rows[u][:, :, CID:CID + 1], tokid[:, bass.ds(gc * G, G)].unsqueeze(2), ACT.Copy).then_inc(s_x2_rows, 1)
                    act.wait_ge(s_z_ps, gc + 1)
                    affine4(zT, ps_d, mod_c[u][:, 1, :], vec[:, 7:8]).then_inc(s_zT_sb, 1)
            run_steps(act, step)

            def expert(q, u):
                return table_entry(0, q * 3 + u, mybir.EngineType.Activation, NE - 1)

            def z_copy(q, u, r):
                a(w1t[u][:, :], w1s[:, bass.ds(r, 1), :].rearrange("p a f -> p (a f)"), ACT.Copy)
                a(b1t[u][:, :], b1s[:, bass.ds(r, 1), :].rearrange("p a k -> p (a k)"), ACT.Copy)
                act.wait_ge(s_zt2_ps, q * 3 + (u + 1))
                a(zt[u][:, :], ps_z, ACT.Copy).then_inc(s_zt2_sb[u], 1)

            def gelu(q, u, r):
                act.wait_ge(s_hb_sb, q * 3 + (u + 1))
                a(b2t[u][:, :], b2s[:, bass.ds(r, 1), :].rearrange("p a f -> p (a f)"), ACT.Copy)
                a(hg[u], hb[u], ACT.Gelu).then_inc(s_hg_sb[u], 1)

            act.preload_act_table(ACT.Gelu)
            act.wait_ge(s_tail_row, 1)
            for ex in range(1, NE, 2):
                r = tail_of(ex, mybir.EngineType.Activation)
                act.dma_start(rows_dram[bass.ds(r, P), :], tail[:, :]).then_inc(s_tails_done, 16)
            act.wait_ge(s_tab_sb, 1)
            act.wait_ge(s_b1_ps, 1)
            a(b1s[:, :, :].rearrange("p e k -> p (e k)"), ps_h[0][:, 0:NE * FK], ACT.Copy).then_inc(s_b1_sb, 1)
            act.wait_ge(s_b1_sb, 1)
            z_copy(0, 0, expert(0, 0))
            with act.Fori(0, NS // 3 - 1) as q:
                for u in range(3):
                    following = (q, u + 1) if u < 2 else (q + 1, 0)
                    r_next = expert(*following)
                    z_copy(*following, r_next)
                    if u == 0:
                        r = expert(q, 0)
                    gelu(q, u, r)
                    r = r_next
            q = NS // 3 - 1
            r = expert(q, 0)
            for u in range(3):
                if u < 2:
                    r_next = expert(q, u + 1)
                    z_copy(q, u + 1, r_next)
                gelu(q, u, r)
                r = r_next

        @block.vector
        def _(dve):
            v = nc.vector
            tt, ts = v.tensor_tensor, v.tensor_scalar

            chain = [0]

            def then(ins):
                chain[0] += 1
                ins.then_inc(s_dchain, 1)
                dve.wait_ge(s_dchain, chain[0])

            dve.wait_ge(s_consts, 1)
            v.tensor_copy(base[:, :], ecap[:, :]).then_inc(s_base_sb, 1)
            dve.wait_ge(s_scal_ld, 32)
            then(ts(decayt[:, :], ones[:, :], scal[:, 0:1], None, ALU.mult))
            then(ts(scal[:, 2:3], scal[:, 1:2], -1.0, 1.0, ALU.mult, ALU.add))
            dve.wait_ge(s_setT_sb, 1)
            dve.wait_ge(s_sty_sb, 1)
            tt(styles2[:, :, :], styles, styles, ALU.mult)
            tt(sqT[:, 0, :], matsT[:, 0, :], matsT[:, 0, :], ALU.mult)
            tt(sqT[:, 1:3, :], matsT[:, 3:5, :], matsT[:, 3:5, :], ALU.mult).then_inc(s_sq_sb, 1)
            dve.wait_ge(s_dem_ps, 1)
            ts(var[:, :, :].rearrange("p j b -> p (j b)"), ps_l[:, 0:3 * B], EPS, None, ALU.add).then_inc(s_var_sb, 1)
            dve.wait_ge(s_root_sb, 1)
            then(v.reciprocal(inv[:, :, :], root[:, :, :]))
            then(tt(newt[:, :, :], inv[:, :, :], inv[:, :, :], ALU.mult))
            then(tt(newt[:, :, :], newt[:, :, :], var[:, :, :], ALU.mult))
            then(ts(newt[:, :, :], newt[:, :, :], -0.5, 1.5, ALU.mult, ALU.add))
            tt(demod, inv[:, :, :], newt[:, :, :], ALU.mult).then_inc(s_setup_done, 1)

            def shifted(o1):
                return bass.AP(tensor=U, offset=o1 * G * UW + WRAP - o1,
                               ap=[[NO * G * UW, P], [G * UW - 1, H - NO], [UW, G], [1, H]])

            def heads(ap):
                return ap.rearrange("p (k h) -> p k h", k=G)

            def step(s, u, do_h, do_a, do_b, do_c, do_d):
                ga, gb, gc, gd = s, s - 1, s - 2, s - 3
                kx = kext[1 - u]

                def states(g):
                    dve.wait_ge(s_h_sb, g + 1)
                    for k in range(G):
                        last = v.tensor_tensor_scan(stT[:, k * L:(k + 1) * L], decayt[:, :], hT[:, k * L:(k + 1) * L], 0.0,
                                                    ALU.mult, ALU.add)
                    last.then_inc(s_st_sb, 1)

                def value_products(c):
                    back = (3, 2, 0)[c]
                    if due(gb * NCH - back):
                        dve.wait_ge(s_av_ps, gb * NCH - back)
                    ec = ps_e[:, c * KQ:(c + 1) * KQ, :, :].rearrange("p o k h -> p (o k h)").unsqueeze(2).to_broadcast([P, KQ * G * H, D])
                    vo = bass.AP(tensor=kx, offset=c * KQ * D, ap=[[G * 2 * C, P], [D, KQ], [2 * C, G], [1, C]])
                    tt(av[c][:, :, :].rearrange("p o (kh d) -> p (o kh) d", d=D), ec, vo, ALU.mult).then_inc(s_av_sb, 1)
                if do_b:
                    dve.wait_ge(s_kext_sb, gb + 1)
                    q = bass.AP(tensor=kx, offset=0, ap=[[G * 2 * C, P], [0, NLO], [2 * C, G], [1, C]])
                    qo = bass.AP(tensor=kx, offset=0, ap=[[G * 2 * C, P], [D, NLO], [2 * C, G], [1, C]])
                    tt(qk[:, 0:NLO, :, :], q, qo, ALU.mult).then_inc(s_qk_sb, 1)
                if do_a:
                    dve.wait_ge(s_y_aff, ga + 1)
                    ts(ypad[:, :, 1:L + 1], tiles(yaff[:, :]), CLAMP, -CLAMP, ALU.min, ALU.max).then_inc(s_y_clip, 1)
                if do_b:
                    dve.wait_ge(s_qk_sb, gb + 1)
                    v.reduce_sum(U[:, 0:NLO, :, WRAP:UW], qk[:, 0:NLO, :, :].rearrange("p o k (h d) -> p (o k) h d", d=D), AX)
                if do_a:
                    dve.wait_ge(s_y_mix, ga + 1)
                    v.scalar_tensor_tensor(tiles(inp[:, :]), ypad[:, :, 0:L], scal[:, 2:3], tiles(ymix[:, :]),
                                           ALU.mult, ALU.add).then_inc(s_inp_sb, 1)
                if do_a and not do_c:
                    states(ga)
                if do_b:
                    dve.wait_ge(s_qkhi_sb, gb + 1)
                    v.reduce_sum(U[:, NLO:NO, :, WRAP:UW], qk[:, NLO:NO, :, :].rearrange("p o k (h d) -> p (o k) h d", d=D), AX).then_inc(s_u_sb, 1)
                lg = ps_l[:, 0:G * NE].rearrange("p (k e) -> p k e", k=G)
                if do_d:
                    dve.wait_ge(s_lg_ps, gd + 1)
                    v.reduce_max(lmax[:, :], lg, AX).then_inc(s_lmax_sb, 1)
                if do_a and do_c:
                    states(ga)
                if do_d:
                    dve.wait_ge(s_lmax_sb, gd + 1)
                    tt(ld[:, :, :], lg, lmax[:, :].unsqueeze(2).to_broadcast([P, G, NE]), ALU.subtract).then_inc(s_ld_sb, 1)
                if do_b:
                    dve.wait_ge(s_u_sb, gb + 1)
                    v.tensor_copy(U[:, 1:WRAP, :, 0:WRAP], U[:, 1:WRAP, :, H:UW]).then_inc(s_u_wrap, 1)
                    v.reduce_max(heads(mx[:, 0, :]), U[:, :, :, WRAP:UW].rearrange("p o k h -> p k h o"), AX)
                if do_d:
                    dve.wait_ge(s_ld_sb, gd + 1)
                    ts(hit[:, :, :], ld[:, :, :], 0.0, -float(2 * NE), ALU.is_equal, ALU.mult).then_inc(s_hit_sb, 1)
                if do_b:
                    dve.wait_ge(s_u_wrap, gb + 1)
                    v.reduce_max(heads(mx[:, 1, :]), shifted(1).rearrange("p o k h -> p k h o"), AX).then_inc(s_m_part, 1)
                if do_d:
                    dve.wait_ge(s_hit_sb, gd + 1)
                    tt(score[:, :, :], hit[:, :, :], iota_e[:, :, :], ALU.add).then_inc(s_score_sb, 1)
                if do_b:
                    dve.wait_ge(s_m_part, gb + 1)
                    tt(mx[:, 2, :], mx[:, 0, :], mx[:, 1, :], ALU.max).then_inc(s_m_sb, 1)
                if do_d:
                    dve.wait_ge(s_score_sb, gd + 1)
                    v.tensor_reduce(smin[:, :], score[:, :, :], AX, ALU.min).then_inc(s_smin_sb, 1)
                if do_b:
                    dve.wait_ge(s_m_sb, gb + 1)
                    if due(gb):
                        dve.wait_ge(s_e3_sb, gb)
                    m = heads(mx[:, 2, :]).unsqueeze(1)
                    tt(sc[:, 0:NO, :, :], U[:, :, :, WRAP:UW], m.to_broadcast([P, NO, G, H]), ALU.subtract).then_inc(s_sclo_sb, 1)
                    tt(sc[:, NO:H, :, :][:, ::-1, :, :], shifted(1), m.to_broadcast([P, H - NO, G, H]), ALU.subtract).then_inc(s_sc_sb, 1)
                if do_d:
                    dve.wait_ge(s_smin_sb, gd + 1)
                    tt(onehot[:, 0:G, :], score[:, :, :], smin[:, :].unsqueeze(2).to_broadcast([P, G, NE]), ALU.is_equal).then_inc(s_oh_sb, 1)
                if do_b:
                    dve.wait_ge(s_elo_sb, gb + 1)
                    value_products(0)
                if do_c:
                    dve.wait_ge(s_av_ps, (gc + 1) * NCH)
                    dve.wait_ge(s_rinv_sb, gc + 1)
                    tt(att[:, :].rearrange("p (h d) -> p h d", d=D), ps_av[:, :].rearrange("p (h d) -> p h d", d=D),
                       rinv[:, :].unsqueeze(2).to_broadcast([P, G * H, D]), ALU.mult).then_inc(s_att_sb, 1)
                if do_b:
                    dve.wait_ge(s_e_sb, gb + 1)
                    v.reduce_sum(heads(esum[:, :]), ps_e[:, :, :, :].rearrange("p o k h -> p k h o"), AX).then_inc(s_esum_sb, 1)
                if do_d:
                    dve.wait_ge(s_le_sb, gd + 1)
                    v.reduce_sum(lsum[:, :], le[:, :, :], AX).then_inc(s_lsum_sb, 1)
                    dve.wait_ge(s_rank_ps, gd + 1)
                    rk = ps_l[:, 64:64 + G * NE].rearrange("p (k e) -> p k e", k=G)
                    dve.wait_ge(s_base_sb, gd + 1)
                    tt(rank[:, :, :], rk, base[:, :].unsqueeze(1).to_broadcast([P, G, NE]), ALU.add).then_inc(s_rank_sb, 1)
                    dve.wait_ge(s_rank_sb, gd + 1)
                    tt(mine[:, :, :], rank[:, :, :], onehot[:, 0:G, :], ALU.mult).then_inc(s_mine_sb, 1)
                    tt(base[:, :], base[:, :], ps_l[:, 64 + G * NE:64 + (G + 1) * NE], ALU.add).then_inc(s_base_sb, 1)
                    dve.wait_ge(s_mine_sb, gd + 1)
                    v.reduce_sum(posf[:, :], mine[:, :, :], AX).then_inc(s_posf_sb, 1)
                    dve.wait_ge(s_lsum_sb, gd + 1)
                    dve.wait_ge(s_rows_free, gd + 1)
                    v.reciprocal(rows[1 - u][:, :, CWT:CWT + 1], lsum[:, :].unsqueeze(2))
                    dve.wait_ge(s_posf_sb, gd + 1)
                    v.tensor_copy(pos[1 - u][:, :], posf[:, :]).then_inc(s_pos_sb, 1)
                if do_b:
                    value_products(1)
                    dve.wait_ge(s_esum_sb, gb + 1)
                    v.reciprocal(rinv[:, :], esum[:, :]).then_inc(s_rinv_sb, 1)
                    value_products(2)
            run_steps(dve, step)

            dve.wait_ge(s_base_sb, NG + 1)
            v.tensor_copy(tail_row[:, :], base[:, :]).then_inc(s_tail_row, 1)
            then(tt(cnt[:, :], base[:, :], ecap[:, :], ALU.subtract))
            then(tt(more[:, :, :], cnt[:, :].unsqueeze(2).to_broadcast([P, NE, B]), iota_k[:, :, :], ALU.is_gt))
            then(v.reduce_sum(ntile[:, :], more[:, :, :], AX))
            then(v.tensor_tensor_scan(cum[:, :], ones[:, 0:NE], ntile[:, :], 0.0, ALU.mult, ALU.add))
            then(tt(past[:, :, :], cum[:, :].unsqueeze(1).to_broadcast([P, NS, NE]), iota_i[:, :, :], ALU.is_le))
            tt(pastn[:, :, :], past[:, :, :], ntile[:, :].unsqueeze(1).to_broadcast([P, NS, NE]), ALU.mult)
            then(v.reduce_sum(tabf[:, 0, :], past[:, :, :], AX))
            then(v.reduce_sum(tabf[:, 1, :], pastn[:, :, :], AX))
            then(tt(tabf[:, 1, :], iota_i[:, :, 0], tabf[:, 1, :], ALU.subtract))
            then(ts(tabf[:, 2, :], tabf[:, 0, :], float(CAP), None, ALU.mult))
            then(v.scalar_tensor_tensor(tabf[:, 1, :], tabf[:, 1, :], float(P), tabf[:, 2, :], ALU.mult, ALU.add))
            then(ts(tabf[:, 1, :], tabf[:, 1, :], float(NE * CAP), None, ALU.min))
            then(ts(tabf[:, 0, :], tabf[:, 0, :], float(NE - 1), None, ALU.min))
            v.tensor_copy(tab[:, :, :], tabf[:, 0:2, :]).then_inc(s_tab_sb, 1)
            dve.wait_ge(s_tab_sb, 1)
            dve.wait_ge(s_exp_ld, 64)

            def bias_up(q, u):
                i = q * 3 + u
                dve.wait_ge(s_h2_ps, i + 1)
                b = b1t[u][:, :].unsqueeze(2).to_broadcast([P, FK, P])
                tt(hb[u].rearrange("p (k t) -> p k t", k=FK), ps_h[u][:, :].rearrange("p (k t) -> p k t", k=FK), b, ALU.add).then_inc(s_hb_sb, 1)

            def finish(q, u, first=False):
                i = q * 3 + u
                dve.wait_ge(s_y2_ps, i + 1)
                tt(yb[u], ps_y[u], b2t[u][:, :], ALU.add).then_inc(s_yb_sb, 1)
                if not first:
                    dve.wait_ge(o_out[u], q * 16)
                dve.wait_ge(rest_ld[u], q * 16 + 16)
                v.tensor_copy(oid[u][:, :], rest[u][:, CID - C:CID - C + 1]).then_inc(s_oid_sb, 1)
                dve.wait_ge(s_yb_sb, i + 1)
                v.scalar_tensor_tensor(orow[u], yb[u], rest[u][:, CWT - C:CWT - C + 1], rest[u][:, 0:C],
                                       ALU.mult, ALU.add).then_inc(s_orow_sb, 1)

            def tile_steps(q, first=False):
                for u in range(3):
                    if u < 2:
                        finish(q - 1, u + 1, first)
                    else:
                        finish(q, 0)
                    bias_up(q, u)

            bias_up(0, 0)
            bias_up(0, 1)
            finish(0, 0, True)
            bias_up(0, 2)
            tile_steps(1, True)
            with dve.Fori(2, NS // 3) as q:
                tile_steps(q)
            q = NS // 3 - 1
            finish(q, 1)
            finish(q, 2)


_INS = ['x', 'cond_512', 'L0_cond_weight', 'L0_cond_bias', 'L0_cond_affine_w', 'L0_cond_affine_b', 'L0_attn_W_in',
        'L0_attn_b_in', 'L0_attn_W_out', 'L0_attn_b_out', 'L0_attn_decay', 'L0_attn_mix', 'L0_cond2_k_aff_w',
        'L0_cond2_k_aff_b', 'L0_cond2_k_w', 'L0_cond2_k_b', 'L0_cond2_o_aff_w', 'L0_cond2_o_aff_b', 'L0_cond2_o_w',
        'L0_cond2_o_b', 'L0_ffn_gate_w', 'L0_ffn_w1', 'L0_ffn_b1', 'L0_ffn_w2', 'L0_ffn_b2']


def kernel(**inputs):
    import numpy as np
    import concourse.bacc as bacc
    from concourse.bass_utils import run_bass_kernel_spmd

    nc = bacc.Bacc("TRN2", target_bir_lowering=False, num_devices=1)
    arrays, args = {}, []
    for name in _INS:
        a = np.ascontiguousarray(inputs[name])
        a = a.reshape(a.shape or (1,))
        arrays[f"in_{name}_dram"] = a
        args.append(nc.dram_tensor(f"in_{name}_dram", a.shape, mybir.dt.from_np(a.dtype), kind="ExternalInput").ap())
    shape = tuple(inputs['x'].shape)
    args.append(nc.dram_tensor("out_0_dram", shape, mybir.dt.float32, kind="ExternalOutput").ap())
    adaln_attn_ffn(nc, *args)
    r = run_bass_kernel_spmd(nc, [arrays], core_ids=[0])
    return r.results[0]["out_0_dram"]
```
